# Optimizing a Trainium2 kernel written in Bass

```python
import numpy as np
import jax
import jax.numpy as jnp

def _softmax(x, axis=-1):
    return jax.nn.softmax(x, axis=axis)

def _gelu(x):
    return jax.nn.gelu(x, approximate=True)

def _silu(x):
    return jax.nn.silu(x)

def _sigmoid(x):
    return jax.nn.sigmoid(x)

def _layernorm(x, axis=-1, eps=1e-05):
    m = jnp.mean(x, axis=axis, keepdims=True)
    v = jnp.var(x, axis=axis, keepdims=True)
    return (x - m) / jnp.sqrt(v + eps)

def _scatter_add(tgt, idx, src, axis=0):
    return tgt.at[idx].add(src)

def _segment_sum(src, seg, n):
    return jax.ops.segment_sum(src, seg, n)
kernel_name = 'mk_decoder_postln_d1_seqx_r8_ed2072'

def setup_inputs(seed: int=0):
    np.random.seed(seed)
    _w = jnp.asarray

    def _rec_inputs():
        import jax
        import jax.numpy as jnp
        _rk = jax.random.key(seed)
        x = -0.0002928 + 1 * jax.random.normal(jax.random.fold_in(_rk, 1), (16, 256, 128), jnp.float32)
        _lenS = 256 - jax.random.randint(jax.random.fold_in(_rk, 7), (16,), 0, max(1, 256 // 4) + 1, jnp.int32)
        _lenS2 = 1601 - jax.random.randint(jax.random.fold_in(_rk, 8), (16,), 0, max(1, 1601 // 4) + 1, jnp.int32)
        _ctx_1024P = jax.random.normal(jax.random.fold_in(_rk, 11), (16, 16, 128), jnp.float32)
        _ctx_1024c = jax.random.dirichlet(jax.random.fold_in(_rk, 511), 0.3 * jnp.ones((16,), jnp.float32), (16, 1601))
        _ctx_1024t = jnp.einsum('bsk,bkd->bsd', _ctx_1024c, _ctx_1024P)
        _ctx_1024t = _ctx_1024t * jax.lax.rsqrt(jnp.mean(jnp.square(_ctx_1024t)) + 1e-12) * 0.953939
        ctx_1024 = -1.39393e-06 + 0.999914 * (_ctx_1024t + 0.3 * jax.random.normal(jax.random.fold_in(_rk, 611), (16, 1601, 128), jnp.float32))
        fside_BxSxS2_0 = jax.random.uniform(jax.random.fold_in(_rk, 12), (16, 256, 1601), jnp.float32, 0.0, 1)
        _validS = jnp.arange(256)[None, :] < _lenS[:, None]
        _validS2 = jnp.arange(1601)[None, :] < _lenS2[:, None]
        _causal = jnp.tril(jnp.ones((256, 256), dtype=bool))
        mask_BxSxS2_ik1 = jnp.where(jnp.broadcast_to(_validS2[:, None, :], (16, 256, 1601)), 1, 0).astype(jnp.int32)
        return (x, ctx_1024, fside_BxSxS2_0, mask_BxSxS2_ik1)
    x, ctx_1024, fside_BxSxS2_0, mask_BxSxS2_ik1 = _rec_inputs()

    def _L0_attn_setup():
        import jax, jax.numpy as jnp
        import numpy as np
        INV_SQRT2 = 0.7071067811865476

        def _haar_wavedec(x, level):
            details = []
            a = x
            for _ in range(level):
                e, o = (a[:, :, 0::2, :], a[:, :, 1::2, :])
                details.append((e - o) * INV_SQRT2)
                a = (e + o) * INV_SQRT2
            return [a] + details[::-1]

        def _haar_idwt_step(a, d):
            e = (a + d) * INV_SQRT2
            o = (a - d) * INV_SQRT2
            B, H, Lh, Dh = a.shape
            return jnp.stack([e, o], axis=3).reshape(B, H, 2 * Lh, Dh)
        key = jax.random.key(seed)
        ks = jax.random.split(key, 6)
        B, L, D, H, M = (8, 512, 128, 16, 3)
        Dh = D // H
        return {'query': jax.random.normal(ks[0], (B, L, D), jnp.float32), 'W_qkv': jax.random.normal(ks[1], (3 * D, D), jnp.float32) * 0.02, 'b_qkv': jnp.zeros((3 * D,), jnp.float32), 'W_out': jax.random.normal(ks[2], (D, D), jnp.float32) * 0.02, 'b_out': jnp.zeros((D,), jnp.float32), 'weight_q': jax.random.normal(ks[3], (H, M, Dh), jnp.float32), 'weight_v': jax.random.normal(ks[4], (H, M, Dh), jnp.float32)}
    _L0_attn_all = _L0_attn_setup()
    _L0_attn_in = {k: v for k, v in _L0_attn_all.items() if k in ('W_qkv', 'b_qkv', 'W_out', 'b_out', 'weight_q', 'weight_v')}
    del _L0_attn_all

    def _L0_xattn_setup():
        import jax, jax.numpy as jnp
        import numpy as np
        NUM_HEADS = 16
        HIDDEN = 128
        B, S = (2, 256)

        def _split_heads(x, H):
            b, s, d = x.shape
            return x.reshape(b, s, H, d // H).transpose(0, 2, 1, 3)
        key = jax.random.key(seed)
        ks = jax.random.split(key, 14)
        D = HIDDEN
        scale = 1.0 / np.sqrt(D)
        inp = {'query': jax.random.normal(ks[0], (B, S, D), jnp.float32), 'key_in': jax.random.normal(ks[1], (B, S, D), jnp.float32), 'value': jax.random.normal(ks[2], (B, S, D), jnp.float32), 'group_prob': jax.random.uniform(ks[3], (B, S, S), jnp.float32), 'mask': jax.random.randint(ks[4], (B, S, S), 0, 2, jnp.int32), 'wq_k': jax.random.normal(ks[5], (D, D), jnp.float32) * scale, 'wq_b': jnp.zeros((D,), jnp.float32), 'wk_k': jax.random.normal(ks[6], (D, D), jnp.float32) * scale, 'wk_b': jnp.zeros((D,), jnp.float32), 'wv_k': jax.random.normal(ks[7], (D, D), jnp.float32) * scale, 'wv_b': jnp.zeros((D,), jnp.float32), 'wo_k': jax.random.normal(ks[8], (D, D), jnp.float32) * scale, 'wo_b': jnp.zeros((D,), jnp.float32)}
        return inp
    _L0_xattn_all = _L0_xattn_setup()
    _L0_xattn_in = {k: v for k, v in _L0_xattn_all.items() if k in ('wq_k', 'wq_b', 'wk_k', 'wk_b', 'wv_k', 'wv_b', 'wo_k', 'wo_b')}
    del _L0_xattn_all

    def _L0_ffn_setup():
        import jax, jax.numpy as jnp
        import numpy as np
        B, L, D = (2, 256, 128)
        E = 15
        H = D * 1
        K = 3
        T = 1.0
        key = jax.random.key(seed)
        ks = jax.random.split(key, 12)
        s = 0.02
        return {'x': jax.random.normal(ks[0], (B, L, D), dtype=jnp.float32), 'router_W': jax.random.normal(ks[1], (D, E), dtype=jnp.float32) * s, 'router_b': jnp.zeros((E,), dtype=jnp.float32), 'sW1': jax.random.normal(ks[2], (D, H), dtype=jnp.float32) * s, 'sb1': jnp.zeros((H,), dtype=jnp.float32), 'sW2': jax.random.normal(ks[3], (H, D), dtype=jnp.float32) * s, 'sb2': jnp.zeros((D,), dtype=jnp.float32), 'eW1': jax.random.normal(ks[4], (E, D, H), dtype=jnp.float32) * s, 'eb1': jnp.zeros((E, H), dtype=jnp.float32), 'eW2': jax.random.normal(ks[5], (E, H, D), dtype=jnp.float32) * s, 'eb2': jnp.zeros((E, D), dtype=jnp.float32)}
    _L0_ffn_all = _L0_ffn_setup()
    _L0_ffn_in = {k: v for k, v in _L0_ffn_all.items() if k in ('router_W', 'router_b', 'sW1', 'sb1', 'sW2', 'sb2', 'eW1', 'eb1', 'eW2', 'eb2')}
    del _L0_ffn_all
    return {'x': x, 'ctx_1024': ctx_1024, 'fside_BxSxS2_0': fside_BxSxS2_0, 'mask_BxSxS2_ik1': mask_BxSxS2_ik1, 'L0_attn_W_qkv': _L0_attn_in['W_qkv'], 'L0_attn_b_qkv': _L0_attn_in['b_qkv'], 'L0_attn_W_out': _L0_attn_in['W_out'], 'L0_attn_b_out': _L0_attn_in['b_out'], 'L0_attn_weight_q': _L0_attn_in['weight_q'], 'L0_attn_weight_v': _L0_attn_in['weight_v'], 'L0_xattn_wq_k': _L0_xattn_in['wq_k'], 'L0_xattn_wq_b': _L0_xattn_in['wq_b'], 'L0_xattn_wk_k': _L0_xattn_in['wk_k'], 'L0_xattn_wk_b': _L0_xattn_in['wk_b'], 'L0_xattn_wv_k': _L0_xattn_in['wv_k'], 'L0_xattn_wv_b': _L0_xattn_in['wv_b'], 'L0_xattn_wo_k': _L0_xattn_in['wo_k'], 'L0_xattn_wo_b': _L0_xattn_in['wo_b'], 'L0_ffn_router_W': _L0_ffn_in['router_W'], 'L0_ffn_router_b': _L0_ffn_in['router_b'], 'L0_ffn_sW1': _L0_ffn_in['sW1'], 'L0_ffn_sb1': _L0_ffn_in['sb1'], 'L0_ffn_sW2': _L0_ffn_in['sW2'], 'L0_ffn_sb2': _L0_ffn_in['sb2'], 'L0_ffn_eW1': _L0_ffn_in['eW1'], 'L0_ffn_eb1': _L0_ffn_in['eb1'], 'L0_ffn_eW2': _L0_ffn_in['eW2'], 'L0_ffn_eb2': _L0_ffn_in['eb2']}

def reference(x, ctx_1024, fside_BxSxS2_0, mask_BxSxS2_ik1, L0_attn_W_qkv, L0_attn_b_qkv, L0_attn_W_out, L0_attn_b_out, L0_attn_weight_q, L0_attn_weight_v, L0_xattn_wq_k, L0_xattn_wq_b, L0_xattn_wk_k, L0_xattn_wk_b, L0_xattn_wv_k, L0_xattn_wv_b, L0_xattn_wo_k, L0_xattn_wo_b, L0_ffn_router_W, L0_ffn_router_b, L0_ffn_sW1, L0_ffn_sb1, L0_ffn_sW2, L0_ffn_sb2, L0_ffn_eW1, L0_ffn_eb1, L0_ffn_eW2, L0_ffn_eb2):
    import jax
    import jax.numpy as jnp

    def _L0_attn_ref(query, W_qkv, b_qkv, W_out, b_out, weight_q, weight_v):
        import jax, jax.numpy as jnp
        import numpy as np
        INV_SQRT2 = 0.7071067811865476

        def _haar_wavedec(x, level):
            details = []
            a = x
            for _ in range(level):
                e, o = (a[:, :, 0::2, :], a[:, :, 1::2, :])
                details.append((e - o) * INV_SQRT2)
                a = (e + o) * INV_SQRT2
            return [a] + details[::-1]

        def _haar_idwt_step(a, d):
            e = (a + d) * INV_SQRT2
            o = (a - d) * INV_SQRT2
            B, H, Lh, Dh = a.shape
            return jnp.stack([e, o], axis=3).reshape(B, H, 2 * Lh, Dh)
        B, L, D = query.shape
        H, M, Dh = weight_q.shape
        qkv = query @ W_qkv.T + b_qkv
        q = qkv[..., :D].reshape(B, L, H, Dh).transpose(0, 2, 1, 3)
        v = qkv[..., 2 * D:].reshape(B, L, H, Dh).transpose(0, 2, 1, 3)
        cq = _haar_wavedec(q, M)
        cv = _haar_wavedec(v, M)
        prod = []
        for j in range(M):
            wq = weight_q[None, :, j, None, :]
            wv = weight_v[None, :, j, None, :]
            prod.append(cq[j] * wq * (cv[j] * wv))
        prod.append(cq[M] * cv[M])
        a = prod[0]
        for d in prod[1:]:
            a = _haar_idwt_step(a, d)
        out = a.transpose(0, 2, 1, 3).reshape(B, L, D)
        return out @ W_out.T + b_out

    def _L0_xattn_ref(query, key_in, value, group_prob, mask, wq_k, wq_b, wk_k, wk_b, wv_k, wv_b, wo_k, wo_b):
        import jax, jax.numpy as jnp
        import numpy as np
        NUM_HEADS = 16
        HIDDEN = 128
        B, S = (2, 256)

        def _split_heads(x, H):
            b, s, d = x.shape
            return x.reshape(b, s, H, d // H).transpose(0, 2, 1, 3)
        H = NUM_HEADS
        dh = query.shape[-1] // H
        q = _split_heads(query @ wq_k + wq_b, H)
        k = _split_heads(key_in @ wk_k + wk_b, H)
        v = _split_heads(value @ wv_k + wv_b, H)
        logits = jnp.einsum('bhqd,bhkd->bhqk', q, k) / jnp.sqrt(jnp.asarray(dh, q.dtype))
        neg = (1.0 - mask.astype(q.dtype)) * -1000000000.0
        logits = logits + neg[:, None, :, :]
        attn = jax.nn.softmax(logits, axis=-1)
        attn = attn * group_prob[:, None, :, :]
        out = jnp.einsum('bhqk,bhkd->bhqd', attn, v)
        out = out.transpose(0, 2, 1, 3).reshape(query.shape[0], -1, H * dh)
        return out @ wo_k + wo_b

    def _L0_ffn_ref(x, router_W, router_b, sW1, sb1, sW2, sb2, eW1, eb1, eW2, eb2):
        import jax, jax.numpy as jnp
        import numpy as np
        B, L, D = (2, 256, 128)
        E = 15
        H = D * 1
        K = 3
        T = 1.0
        b, l, d = x.shape
        n = b * l
        xt = x.reshape(n, d)
        shared = jax.nn.relu(xt @ sW1 + sb1) @ sW2 + sb2
        logits = xt @ router_W + router_b
        probs = jax.nn.softmax(logits / T, axis=-1)
        top_p, top_i = jax.lax.top_k(probs, K)
        cw = jnp.zeros((n, E), dtype=probs.dtype)
        cw = cw.at[jnp.arange(n)[:, None], top_i].set(top_p)
        h = jax.nn.relu(jnp.einsum('nd,edh->neh', xt, eW1) + eb1)
        ye = jnp.einsum('neh,ehd->ned', h, eW2) + eb2
        routed = jnp.einsum('ned,ne->nd', ye, cw)
        return (shared + routed).reshape(b, l, d)
    x = _layernorm(x + _L0_attn_ref(x, L0_attn_W_qkv, L0_attn_b_qkv, L0_attn_W_out, L0_attn_b_out, L0_attn_weight_q, L0_attn_weight_v), axis=-1)
    x = _layernorm(x + _L0_xattn_ref(x, ctx_1024, ctx_1024, fside_BxSxS2_0, mask_BxSxS2_ik1, L0_xattn_wq_k, L0_xattn_wq_b, L0_xattn_wk_k, L0_xattn_wk_b, L0_xattn_wv_k, L0_xattn_wv_b, L0_xattn_wo_k, L0_xattn_wo_b), axis=-1)
    x = _layernorm(x + _L0_ffn_ref(x, L0_ffn_router_W, L0_ffn_router_b, L0_ffn_sW1, L0_ffn_sb1, L0_ffn_sW2, L0_ffn_sb2, L0_ffn_eW1, L0_ffn_eb1, L0_ffn_eW2, L0_ffn_eb2), axis=-1)
    return x

_drawn_inputs = setup_inputs


def setup_inputs(seed=0):
    import zlib

    import numpy as np

    out = dict(_drawn_inputs(seed))
    spreads = {'L0_attn_b_qkv': (0.0, 0.719),
     'L0_attn_b_out': (0.0, 0.44),
     'L0_xattn_wq_b': (0.0, 0.8),
     'L0_xattn_wk_b': (0.0, 2.0),
     'L0_xattn_wv_b': (0.0, 0.1),
     'L0_xattn_wo_b': (0.0, 0.1),
     'L0_ffn_router_b': (0.0, 0.8),
     'L0_ffn_sb1': (0.0, 0.591),
     'L0_ffn_sb2': (0.0, 0.1),
     'L0_ffn_eb1': (0.0, 0.8),
     'L0_ffn_eb2': (0.0, 0.528)}
    factors = {'fside_BxSxS2_0': 4.027,
     'L0_attn_W_qkv': 4.002,
     'L0_attn_W_out': 3.513,
     'L0_attn_weight_q': 4.702,
     'L0_attn_weight_v': 4.405,
     'L0_ffn_router_W': 3.887,
     'L0_ffn_eW1': 8.0,
     'L0_ffn_eW2': 8.0}
    for name, (base, spread) in spreads.items():
        noise = np.random.default_rng([zlib.crc32(name.encode()), seed]).standard_normal(out[name].shape)
        drawn = base * np.exp(spread * noise) if base else spread * noise
        out[name] = jnp.asarray(drawn.astype(out[name].dtype))
    for name, factor in factors.items():
        out[name] = (out[name] * factor).astype(out[name].dtype)
    return out
```

```python
from contextlib import ExitStack

import concourse.bass as bass
from concourse import mybir

F32 = mybir.dt.float32
BF16 = mybir.dt.bfloat16
I32 = mybir.dt.int32
ALU = mybir.AluOpType
ACT = mybir.ActivationFunctionType
AX_X = mybir.AxisListType.X
P = 128
EPS = 1e-5
TT = 4
CH = TT * P


class Scope:

    def __init__(self, nc, name):
        self.nc, self.name, self.stack = nc, name, ExitStack()

    def __enter__(self):
        self.stack.__enter__()
        return self

    def __exit__(self, *a):
        return self.stack.__exit__(*a)

    def sb(self, name, shape, dt=F32):
        return self.stack.enter_context(self.nc.sbuf_tensor(f"{self.name}_{name}", shape, dt))

    def ps(self, name, shape, dt=F32):
        return self.stack.enter_context(self.nc.psum_tensor(f"{self.name}_{name}", shape, dt))

    def sem(self, name):
        return self.stack.enter_context(self.nc.semaphore(f"{self.name}_{name}"))


def pass_wait(eng, passed):
    eng.sem_inc(passed, 1)


def row_bcast(vec, n=P):
    return vec.rearrange("(a m) -> a m", a=1).to_broadcast([n, vec.shape[0]])


def column(vec):
    return vec.rearrange("(m a) -> m a", a=1)


def make_identity(pool, ident, zeroed, made):
    pool.memset(ident[:, :], 0.0).then_inc(zeroed, 1)
    pool.wait_ge(zeroed, 1)
    pool.affine_select(out=ident[:, :], in_=ident[:, :], compare_op=ALU.not_equal, fill=1.0,
                       base=0, pattern=[[-1, P]], channel_multiplier=1).then_inc(made, 1)


def wavelet_pass(nc, x, W_qkv, b_qkv, W_out, b_out, weight_q, weight_v, x1_dram):
    B, L, D = x.shape
    H, M, Dh = weight_q.shape
    chunks = B * L // CH
    S = 0.5 ** 0.5
    x_t = x.rearrange("b l d -> (b l) d").rearrange("(c t p) d -> c p t d", t=TT, p=P)
    x1_t = x1_dram.rearrange("(c t p) d -> c p t d", t=TT, p=P)

    with Scope(nc, "wav") as s:
        ident = s.sb("ident", [P, P])
        w_nat = s.sb("w_nat", [P, 3, P])
        w_T = s.sb("w_T", [P, 3, P])
        wqv_rows = s.sb("wqv_rows", [M, 2, P])
        wqv_c = s.sb("wqv_c", [P, 2 * M])
        w_c = s.sb("w_c", [P, M])
        coef = s.sb("coef", [P, M])
        bias_q = s.sb("bias_q", [P, 1])
        bias_v = s.sb("bias_v", [P, 1])
        bias_o = s.sb("bias_o", [P, P])
        xin = [s.sb(f"xin{u}", [P, TT, P]) for u in range(2)]
        xT = [s.sb(f"xT{u}", [P, CH]) for u in range(2)]
        qv = [s.sb(f"qv{u}", [P, 2, CH]) for u in range(2)]
        a1 = s.sb("a1", [P, 2, CH // 2])
        d1 = s.sb("d1", [P, 2, CH // 2])
        a2 = s.sb("a2", [P, 2, CH // 4])
        d2 = s.sb("d2", [P, 2, CH // 4])
        a3 = s.sb("a3", [P, 2, CH // 8])
        d3 = s.sb("d3", [P, 2, CH // 8])
        p0 = s.sb("p0", [P, CH // 8])
        p1 = s.sb("p1", [P, CH // 8])
        p2 = s.sb("p2", [P, CH // 4])
        p3 = s.sb("p3", [P, CH // 2])
        r1 = s.sb("r1", [P, CH // 4])
        r2 = s.sb("r2", [P, CH // 2])
        mixed = [s.sb(f"mixed{u}", [P, CH]) for u in range(2)]
        y = s.sb("y", [P, TT, P])
        stats = s.sb("stats", [P, TT, 6])
        mv = s.sb("mv", [P, TT, 2])
        std = s.sb("std", [P, TT])
        rstd = s.sb("rstd", [P, TT])
        eps = s.sb("eps", [P, 1])
        x1 = [s.sb(f"x1{u}", [P, TT, P]) for u in range(2)]
        ps_w = s.ps("ps_w", [P, 512])
        ps_x = s.ps("ps_x", [P, CH])
        ps_q = s.ps("ps_q", [P, CH])
        ps_v = s.ps("ps_v", [P, CH])
        ps_o = s.ps("ps_o", [P, CH])

        w_loaded, x_loaded = s.sem("w_loaded"), [s.sem(f"x_loaded{u}") for u in range(2)]
        zeroed, ident_made, eps_set = s.sem("zeroed"), s.sem("ident_made"), s.sem("eps_set")
        wT_ready, wT_copied = s.sem("wT_ready"), s.sem("wT_copied")
        x_free = s.sem("x_free")
        xT_ready, xT_copied = s.sem("xT_ready"), s.sem("xT_copied")
        qv_ready, qv_copied = s.sem("qv_ready"), s.sem("qv_copied")
        mixed_ready, o_ready = s.sem("mixed_ready"), s.sem("o_ready")
        step = s.sem("step")
        var_ready, std_ready, x1_ready = s.sem("var_ready"), s.sem("std_ready"), s.sem("x1_ready")
        rstd_ready, wqv_copied = s.sem("rstd_ready"), s.sem("wqv_copied")
        passed = s.sem("passed")
        x1_free = s.sem("x1_free")
        stored = [s.sem(f"stored{u}") for u in range(2)]
        block = s.stack.enter_context(nc.Block())
        n_w = 16 * 8

        @block.sync
        def _(sp):
            loads = [(w_nat[:, 0, :], W_qkv[0:D, :]), (w_nat[:, 1, :], W_qkv[2 * D:3 * D, :]), (w_nat[:, 2, :], W_out),
                     (bias_q[:, :], column(b_qkv[0:D])), (bias_v[:, :], column(b_qkv[2 * D:3 * D])),
                     (bias_o[:, :], row_bcast(b_out))]
            for k, w in enumerate((weight_q, weight_v)):
                loads.append((wqv_rows[:, k, :].rearrange("m (h d) -> m h d", h=H), w.rearrange("h m d -> m h d")))
            for dst, src in loads:
                sp.dma_start(dst, src).then_inc(w_loaded, 16)
            with sp.Fori(0, chunks // 2) as i:
                for u in range(2):
                    c = i * 2 + u
                    sp.wait_ge(x_free, c + 1)
                    sp.dma_start(xin[u][:, :, :], x_t[bass.ds(c, 1)].rearrange("c p t d -> (c p) t d")).then_inc(x_loaded[u], 16)

        @block.gpsimd
        def _(pool):
            make_identity(pool, ident, zeroed, ident_made)
            pool.memset(eps[:, :], EPS).then_inc(eps_set, 1)
            pool.sem_inc(x1_free, 2)
            with pool.Fori(0, chunks // 2) as i:
                for u in range(2):
                    c = i * 2 + u
                    pool.wait_ge(x1_ready, c + 1)
                    pool.dma_start(x1_t[bass.ds(c, 1)].rearrange("c p t d -> (c p) t d"), x1[u][:, :, :]).then_inc(stored[u], 16)
                    pool.wait_ge(stored[u], i * 16 + 16)
                    pool.sem_inc(x1_free, 1)

        @block.tensor
        def _(pe):
            pe.wait_ge(w_loaded, n_w)
            pe.wait_ge(ident_made, 1)
            for k in range(3):
                pe.transpose(ps_w[:, k * P:(k + 1) * P], w_nat[:, k, :], ident[:, :])
            for k in range(2):
                last = pe.transpose(ps_w[:, 3 * P + k * M:3 * P + (k + 1) * M], wqv_rows[:, k, :], ident[0:M, 0:M])
            last.then_inc(wT_ready, 1)
            pe.wait_ge(wT_copied, 1)
            with pe.Fori(0, chunks // 2) as i:
                for u in range(2):
                    c = i * 2 + u
                    pe.wait_ge(x_loaded[u], i * 16 + 16)
                    pe.wait_ge(xT_copied, c)
                    for t in range(TT):
                        last = pe.transpose(ps_x[:, t * P:(t + 1) * P], xin[u][:, t, :], ident[:, :])
                    last.then_inc(xT_ready, 1)
                    pe.wait_ge(xT_copied, c + 1)
                    pe.wait_ge(qv_copied, c * 2)
                    pe.matmul(ps_q[:, :], w_T[:, 0, :], xT[u][:, :], start=True, stop=True).then_inc(qv_ready, 1)
                    pe.matmul(ps_v[:, :], w_T[:, 1, :], xT[u][:, :], start=True, stop=True).then_inc(qv_ready, 1)
                    pe.wait_ge(mixed_ready, c + 1)
                    for t in range(TT):
                        last = pe.matmul(ps_o[:, t * P:(t + 1) * P], mixed[u][:, t * P:(t + 1) * P], w_T[:, 2, :],
                                         start=True, stop=True)
                    last.then_inc(o_ready, 1)

        @block.scalar
        def _(act):
            act.wait_ge(eps_set, 1)
            act.wait_ge(w_loaded, n_w)
            with act.Fori(0, chunks // 2) as i:
                for u in range(2):
                    c = i * 2 + u
                    act.wait_ge(xT_ready, c + 1)
                    act.activation(xT[u][:, :], ps_x[:, :], ACT.Copy).then_inc(xT_copied, 1)
                    act.wait_ge(qv_ready, c * 2 + 1)
                    act.activation(qv[u][:, 0, :], ps_q[:, :], ACT.Identity, bias=bias_q[:, :]).then_inc(qv_copied, 1)
                    act.wait_ge(qv_ready, c * 2 + 2)
                    act.activation(qv[u][:, 1, :], ps_v[:, :], ACT.Identity, bias=bias_v[:, :]).then_inc(qv_copied, 1)
                    act.wait_ge(var_ready, c + 1)
                    act.activation(std[:, :], mv[:, :, 1], ACT.Sqrt, bias=eps[:, :]).then_inc(std_ready, 1)

        @block.vector
        def _(dve):
            dve.wait_ge(w_loaded, n_w)
            dve.wait_ge(wT_ready, 1)
            dve.tensor_copy(wqv_c[:, :], ps_w[:, 3 * P:3 * P + 2 * M]).then_inc(wqv_copied, 1)
            dve.tensor_copy(w_T[:, :, :].rearrange("p k n -> p (k n)"), ps_w[:, 0:3 * P]).then_inc(wT_copied, 1)
            dve.wait_ge(wqv_copied, 1)
            dve.tensor_tensor(w_c[:, :], wqv_c[:, 0:M], wqv_c[:, M:2 * M], ALU.mult).then_inc(step, 1)
            dve.wait_ge(step, 1)
            dve.tensor_scalar(coef[:, 0:2], w_c[:, 0:2], S ** 9, None, ALU.mult).then_inc(step, 1)
            dve.tensor_scalar(coef[:, 2:3], w_c[:, 2:3], S ** 6, None, ALU.mult).then_inc(step, 1)
            dve.sem_inc(x_free, 2)
            STEPS = 19
            with dve.Fori(0, chunks // 2) as i:
                for u in range(2):
                    c = i * 2 + u
                    at = c * STEPS + 3
                    q = qv[u]
                    dve.wait_ge(qv_copied, c * 2 + 2)
                    dve.wait_ge(step, at)
                    dve.tensor_tensor(a1[:, :, :], q[:, :, 0::2], q[:, :, 1::2], ALU.add).then_inc(step, 1)
                    dve.tensor_tensor(d1[:, :, :], q[:, :, 0::2], q[:, :, 1::2], ALU.subtract).then_inc(step, 1)
                    dve.wait_ge(step, at + 1)
                    dve.tensor_tensor(a2[:, :, :], a1[:, :, 0::2], a1[:, :, 1::2], ALU.add).then_inc(step, 1)
                    dve.tensor_tensor(d2[:, :, :], a1[:, :, 0::2], a1[:, :, 1::2], ALU.subtract).then_inc(step, 1)
                    dve.wait_ge(step, at + 3)
                    dve.tensor_tensor(a3[:, :, :], a2[:, :, 0::2], a2[:, :, 1::2], ALU.add).then_inc(step, 1)
                    dve.tensor_tensor(d3[:, :, :], a2[:, :, 0::2], a2[:, :, 1::2], ALU.subtract).then_inc(step, 1)
                    dve.scalar_tensor_tensor(out=p3[:, :], in0=d1[:, 0, :], scalar=S ** 3, in1=d1[:, 1, :],
                                             op0=ALU.mult, op1=ALU.mult).then_inc(step, 1)
                    dve.wait_ge(step, at + 4)
                    dve.scalar_tensor_tensor(out=p2[:, :], in0=d2[:, 0, :], scalar=coef[:, 2:3], in1=d2[:, 1, :],
                                             op0=ALU.mult, op1=ALU.mult).then_inc(step, 1)
                    dve.wait_ge(step, at + 6)
                    dve.scalar_tensor_tensor(out=p1[:, :], in0=d3[:, 0, :], scalar=coef[:, 1:2], in1=d3[:, 1, :],
                                             op0=ALU.mult, op1=ALU.mult).then_inc(step, 1)
                    dve.scalar_tensor_tensor(out=p0[:, :], in0=a3[:, 0, :], scalar=coef[:, 0:1], in1=a3[:, 1, :],
                                             op0=ALU.mult, op1=ALU.mult).then_inc(step, 1)
                    dve.wait_ge(step, at + 10)
                    dve.tensor_tensor(r1[:, 0::2], p0[:, :], p1[:, :], ALU.add).then_inc(step, 1)
                    dve.tensor_tensor(r1[:, 1::2], p0[:, :], p1[:, :], ALU.subtract).then_inc(step, 1)
                    dve.wait_ge(step, at + 12)
                    dve.tensor_tensor(r2[:, 0::2], r1[:, :], p2[:, :], ALU.add).then_inc(step, 1)
                    dve.tensor_tensor(r2[:, 1::2], r1[:, :], p2[:, :], ALU.subtract).then_inc(step, 1)
                    dve.wait_ge(step, at + 14)
                    dve.tensor_tensor(mixed[u][:, 0::2], r2[:, :], p3[:, :], ALU.add).then_inc(step, 1)
                    dve.tensor_tensor(mixed[u][:, 1::2], r2[:, :], p3[:, :], ALU.subtract).then_inc(step, 1)
                    dve.wait_ge(step, at + 16)
                    dve.sem_inc(mixed_ready, 1)
                    bo = bias_o[:, :].unsqueeze(1).to_broadcast([P, TT, P])
                    ps_o_t = ps_o[:, :].rearrange("p (t d) -> p t d", t=TT)
                    dve.wait_ge(o_ready, c + 1)
                    dve.tensor_tensor(y[:, :, :], ps_o_t, bo, ALU.add).then_inc(step, 1)
                    dve.wait_ge(step, at + 17)
                    dve.tensor_tensor(y[:, :, :], y[:, :, :], xin[u][:, :, :], ALU.add).then_inc(step, 1)
                    dve.wait_ge(step, at + 18)
                    dve.sem_inc(x_free, 1)
                    for t in range(TT):
                        last = dve.bn_stats(stats[:, t, :], y[:, t, :])
                    last.then_inc(step, 1)
                    dve.wait_ge(step, at + 19)
                    pass_wait(dve, passed)
                    for t in range(TT):
                        last = dve.bn_aggr(mv[:, t, :], stats[:, t, :])
                    last.then_inc(var_ready, 1)
                    dve.wait_ge(std_ready, c + 1)
                    dve.reciprocal(rstd[:, :], std[:, :]).then_inc(rstd_ready, 1)
                    dve.wait_ge(rstd_ready, c + 1)
                    dve.wait_ge(x1_free, c + 1)
                    for t in range(TT):
                        last = dve.tensor_scalar(x1[u][:, t, :], y[:, t, :], mv[:, t, 0:1], rstd[:, t:t + 1],
                                                 ALU.subtract, ALU.mult)
                    last.then_inc(x1_ready, 1)


class CrossShapes:
    G, HG, DH, LAG, RING = 4, 4, 8, 3, 4
    MASKED = 72
    TOP = 96
    DVE_TILES = (2, 5, 8, 10, 12)


def cross_jobs(first, last):
    jobs = {(g, t): [] for g in range(4) for t in range(13)}
    jobs[0, 1].append("f5")
    jobs[0, 2].append("f6")
    if not first:
        jobs[0, 5].append("den3")
        jobs[0, 7].append("out")
    for g in range(3):
        jobs[g + 1, 5].append(f"den{g}")
    if not last:
        for k in range(4):
            jobs[0, 8 + k].append(f"ctx{k}")
            jobs[1, (1, 2, 3, 4)[k]].append(f"k{k}")
            jobs[1, 7 + k].append(f"v{k}")
        jobs[1, 0].append("x1")
        jobs[1, 6].append("q")
        jobs[2, 0].append("count")
        jobs[2, 1].append("total")
        jobs[2, 2].append("row")
        for k in range(5):
            jobs[3, 4 + 2 * k].append(f"f{k}")
    for g in range(4):
        if not (last and g == 3):
            jobs[g, 9].append("top")
    return jobs


PREPARE = (["ctx0", "ctx1", "ctx2", "ctx3", "x1"] + [f"k{k}" for k in range(4)] + ["q"] + [f"v{k}" for k in range(4)]
           + ["count", "total", "row"] + [f"f{k}" for k in range(5)] + ["top"])


def cross_pass(nc, ctx, gate, mask, wq, bq, wk, bk, wv, bv, wo, bo, x1_dram, y2_dram):
    C = CrossShapes
    B, SK, D = ctx.shape
    SQ = gate.shape[1]
    QT = SQ // P
    KT = -(-SK // P)
    PK = KT * P
    REST = SK - (KT - 1) * P
    HALF = (SK - SK // 2, SK // 2)
    G, HG, DH, LAG, RING, MASKED, TOP = C.G, C.HG, C.DH, C.LAG, C.RING, C.MASKED, C.TOP
    H = G * HG
    UNITS = HG * QT * 2
    NEG = -998244352.0
    SCALE = DH ** -0.5
    VW = H * (DH + 1) + 24
    SLOTS = G * KT
    N_DVE = len(C.DVE_TILES)
    N_POOL = KT - N_DVE

    with Scope(nc, "x") as s:
        ident = s.sb("ident", [P, P])
        ident_bf = s.sb("ident_bf", [P, P], BF16)
        ones = s.sb("ones", [P, P])
        ones_bf = s.sb("ones_bf", [P, 1], BF16)
        spread = s.sb("spread", [P, P])
        w_nat = s.sb("w_nat", [P, 2, P])
        w_sb = s.sb("w_sb", [P, 2, P])
        wv_sb = s.sb("wv_sb", [P, P])
        wo_sb = s.sb("wo_sb", [P, G, P])
        b_rows = s.sb("b_rows", [1, 2, P])
        b_perm = s.sb("b_perm", [1, 2, P])
        b_qk = s.sb("b_qk", [P, 2])
        bv_sb = s.sb("bv_sb", [P, P])
        bo_sb = s.sb("bo_sb", [P, P])
        nat = s.sb("nat", [P, QT, SK])
        nat_int = nat[:, :, :].bitcast(I32)
        ctx_nat = s.sb("ctx_nat", [P, KT, P])
        k_f = ctx_nat[:, :, :].rearrange("p t d -> p (t d)")
        ctx_T = s.sb("ctx_T", [P, PK])
        k_part = [s.sb(f"k_part{n}", [P, PK], BF16) for n in range(3)]
        q_f = s.sb("q_f", [P, SQ])
        q_part = [s.sb(f"q_part{n}", [P, SQ], BF16) for n in range(3)]
        k_aug = s.sb("k_aug", [P, H, PK], BF16)
        q_aug = [s.sb(f"q_aug{u}", [P, H, SQ], BF16) for u in range(2)]
        neg = [s.sb(f"neg{u}", [P, QT, PK], BF16) for u in range(2)]
        gate_T = s.sb("gate_T", [P, KT, SQ])
        values = [s.sb(f"values{u}", [P, KT, VW]) for u in range(2)]
        x1_nat = [s.sb(f"x1_nat{u}", [P, QT, D]) for u in range(2)]
        x1_T = s.sb("x1_T", [P, SQ])
        weights = [s.sb(f"weights{r}", [P, HG, 2 * SQ]) for r in range(RING)]
        swept = [s.sb(f"swept{u}", [P, HALF[0]], BF16) for u in range(2)]
        top2 = s.sb("top2", [P, HG * QT, 2])
        top = s.sb("top", [P, HG * QT])
        top_r = s.sb("top_r", [HG * QT, P])
        top_part = [s.sb(f"top_part{n}", [HG * QT, P], BF16) for n in range(3)]
        seen = s.sb("seen", [P, 2, KT])
        seen_n = s.sb("seen_n", [P, 2])
        whole = s.sb("whole", [P, 2])
        fast = s.sb("fast", [P, 1])
        row_c = s.sb("row_c", [P, KT])
        row_bf = s.sb("row_bf", [KT, P], BF16)
        general = [s.sb(f"general{u}", [P, 1], I32) for u in range(2)]
        o_sb = s.sb("o_sb", [P, 2 * SQ])
        inv = s.sb("inv", [P, SQ])
        o_T = s.sb("o_T", [P, G, SQ])
        y2 = s.sb("y2", [P, QT, D])

        ps_s = [s.ps(f"ps_s{u}", [P, 2 * SQ]) for u in range(2)]
        ps_m = [s.ps(f"ps_m{u}", [P, 1024]) for u in range(2)]
        ps_o = s.ps("ps_o", [P, 2 * SQ])
        ps_misc = s.ps("ps_misc", [P, 512])

        w_loaded, zeroed, made, set_dve = s.sem("w_loaded"), s.sem("zeroed"), s.sem("made"), s.sem("set_dve")
        b_turned, b_ready = s.sem("b_turned"), s.sem("b_ready")
        x1_loaded = [s.sem(f"x1_loaded{u}") for u in range(2)]
        ctx_loaded, mask_loaded, gate_loaded = s.sem("ctx_loaded"), s.sem("mask_loaded"), s.sem("gate_loaded")
        q_loaded = [s.sem(f"q_loaded{u}") for u in range(2)]
        k_loaded = [s.sem(f"k_loaded{g}") for g in range(G)]
        top_loaded = [s.sem(f"top_loaded{g}") for g in range(2)]
        y2_stored = s.sem("y2_stored")
        misc_ready, misc_read = s.sem("misc_ready"), s.sem("misc_read")
        s_ready = s.sem("s_ready")
        exp_ready = s.sem("exp_ready")
        gated_dve, gated_pool = s.sem("gated_dve"), s.sem("gated_pool")
        applied = s.sem("applied")
        o_copied = s.sem("o_copied")
        o_normed = s.sem("o_normed")
        m_ready = s.sem("m_ready")
        m_read = s.sem("m_read")
        top_ready, top_step, top_split = s.sem("top_ready"), s.sem("top_step"), s.sem("top_split")
        part_made = [s.sem(f"part_made{n}") for n in range(3)]
        rest_made = [s.sem(f"rest_made{n}") for n in range(2)]
        neg_made, general_made = s.sem("neg_made"), s.sem("general_made")
        seen_ready, fast_ready, row_ready = s.sem("seen_ready"), s.sem("fast_ready"), s.sem("row_ready")
        y2_ready = s.sem("y2_ready")
        passed = s.sem("passed")
        N_SET = 10

        block = s.stack.enter_context(nc.Block())
        x1_t = x1_dram.rearrange("(b t p) d -> b p t d", t=QT, p=P)
        y2_t = y2_dram.rearrange("(b t p) d -> b p t d", t=QT, p=P)
        gate_t = gate.rearrange("b (t p) k -> b p t k", t=QT)
        mask_t = mask.rearrange("b (t p) k -> b p t k", t=QT)

        def one(ap, b):
            return ap[b] if isinstance(b, int) else ap[bass.ds(b, 1)].rearrange("b p t k -> (b p) t k")

        first_jobs, inner_jobs, last_jobs = cross_jobs(True, False), cross_jobs(False, False), cross_jobs(False, True)
        n_first = sum(len(v) for v in first_jobs.values())
        n_inner = sum(len(v) for v in inner_jobs.values())

        def job_numbers(jobs, b, is_first):
            base = len(PREPARE) if is_first else (b - 1) * n_inner + (len(PREPARE) + n_first)
            number, k = {}, 0
            for slot, names in jobs.items():
                for place in range(len(names)):
                    number[slot, place] = base + k
                    k += 1
            return number, base + k

        def cycles(eng, prologue, cycle, epilogue):
            prologue()
            cycle(0, 0, first_jobs, True, False)
            with eng.Fori(0, (B - 2) // 2) as i:
                for v in range(2):
                    cycle(i * 2 + (1 + v), (1 + v) % 2, inner_jobs, False, False)
            cycle(B - 1, (B - 1) % 2, last_jobs, False, True)
            epilogue()

        def walk(jobs, b, is_first):
            number, _ = job_numbers(jobs, b, is_first)
            for g in range(G):
                for t in range(KT):
                    yield g, t, b * SLOTS + (g * KT + t), [(number[(g, t), k], j) for k, j in enumerate(jobs[g, t])]

        END_JOB = len(PREPARE) + n_first + (B - 2) * n_inner + sum(len(v) for v in last_jobs.values())

        @block.sync
        def _(sp):
            wl = [(w_nat[:, 0, :], wq), (w_nat[:, 1, :], wk), (wv_sb[:, :], wv), (bv_sb[:, :], row_bcast(bv)),
                  (bo_sb[:, :], row_bcast(bo)), (b_rows[:, 0, :], bq.rearrange("(a m) -> a m", a=1)),
                  (b_rows[:, 1, :], bk.rearrange("(a m) -> a m", a=1))]
            for dst, src in wl:
                sp.dma_start(dst, src).then_inc(w_loaded, 16)
            sp.wait_ge(made, 5)
            for j in range(HG):
                sp.dma_start(wo_sb[32 * j:32 * j + DH, :, :],
                             wo.rearrange("(g j d) n -> j d g n", g=G, j=HG)[j]).then_inc(w_loaded, 16)

            def place_k(b, g):
                if not (isinstance(b, int) and b == 0):
                    sp.wait_ge(s_ready, (b - 1) * (2 * SLOTS) + 2 * KT * (g + 1))
                    pass_wait(sp, passed)
                sp.wait_ge(part_made[2], b + 1)
                for c in range(9):
                    sp.dma_start(k_aug[DH * c:DH * c + DH, HG * g:HG * g + HG, :],
                                 k_part[c // 3][32 * g:32 * g + 32, :]).then_inc(k_loaded[g], 16)
                for h in range(HG * g, HG * g + HG):
                    sp.dma_start(k_aug[MASKED:MASKED + 1, h, :], row_bf[:, :]).then_inc(k_loaded[g], 16)

            def place_q(b, u):
                sp.wait_ge(part_made[2], b + 1)
                for g in range(G):
                    for c in range(9):
                        sp.dma_start(q_aug[u][DH * c:DH * c + DH, HG * g:HG * g + HG, :],
                                     q_part[c % 3][32 * g:32 * g + 32, :]).then_inc(q_loaded[u], 16)

            def place_top(b, g, u):
                sp.wait_ge(top_split, b * G + (g + 1))
                for n in range(3):
                    sp.dma_start(q_aug[u][TOP + n:TOP + n + 1, HG * g:HG * g + HG, :], top_part[n][:, :])\
                      .then_inc(top_loaded[g % 2], 16)

            def prologue():
                sp.wait_ge(made, 8)
                sp.wait_ge(set_dve, N_SET)
                place_q(0, 0)
                for g in range(3):
                    place_k(0, g)
                place_top(0, 0, 0)

            def cycle(b, u, jobs, is_first, is_last):
                place_k(b, 3)
                place_top(b, 1, u)
                place_top(b, 2, u)
                if not is_last:
                    place_q(b + 1, 1 - u)
                    place_k(b + 1, 0)
                place_top(b, 3, u)
                if not is_last:
                    place_k(b + 1, 1)
                    place_k(b + 1, 2)
                    place_top(b + 1, 0, 1 - u)

            cycles(sp, prologue, cycle, lambda: None)

        @block.gpsimd
        def _(pool):
            pool.memset(ident[:, :], 0.0).then_inc(zeroed, 1)
            pool.memset(spread[:, :], 0.0).then_inc(zeroed, 1)
            pool.wait_ge(zeroed, 2)
            pool.affine_select(out=ident[:, :], in_=ident[:, :], compare_op=ALU.not_equal, fill=1.0,
                               base=0, pattern=[[-1, P]], channel_multiplier=1).then_inc(made, 1)
            by_head = spread[:, :].rearrange("p (j m) -> p j m", j=HG)
            pool.affine_select(out=by_head, in_=by_head, compare_op=ALU.not_equal, fill=1.0,
                               base=-DH, pattern=[[-32, HG], [0, 32]], channel_multiplier=1).then_inc(made, 1)
            pool.memset(ones[:, :], 1.0).then_inc(made, 1)
            pool.memset(ones_bf[:, :], 1.0).then_inc(made, 1)
            pool.memset(wo_sb[:, :, :], 0.0).then_inc(made, 1)
            pool.memset(k_aug[0:TOP, :, :].bitcast(F32), 0.0).then_inc(made, 1)
            pool.wait_ge(made, 6)
            pool.memset(k_aug[TOP:P, :, :], 1.0).then_inc(made, 1)
            pool.wait_ge(made, 7)
            pool.tensor_copy(ident_bf[:, :], ident[:, :]).then_inc(made, 1)

            def remainder(b, n):
                pool.wait_ge(part_made[n], b + 1)
                pool.tensor_tensor(q_f[:, :], q_f[:, :], q_part[n][:, :], ALU.subtract)
                pool.tensor_tensor(k_f, k_f, k_part[n][:, :], ALU.subtract).then_inc(rest_made[n], 1)

            def prologue():
                remainder(0, 0)
                remainder(0, 1)

            def cycle(b, u, jobs, is_first, is_last):
                for g, t, n, _ in walk(jobs, b, is_first):
                    if t not in C.DVE_TILES:
                        pool.wait_ge(exp_ready, n * 2 + 4)
                        w = weights[(g * KT + t) % RING]
                        pool.tensor_tensor(w[:, :, 0:SQ], w[:, :, SQ:],
                                           gate_T[:, t, :].unsqueeze(1).to_broadcast([P, HG, SQ]), ALU.mult)\
                            .then_inc(gated_pool, 1)
                    if not is_last and (g, t) == (1, 8):
                        remainder(b + 1, 0)
                    if not is_last and (g, t) == (1, 11):
                        remainder(b + 1, 1)

            cycles(pool, prologue, cycle, lambda: None)

        @block.scalar
        def _(act):
            def load_mask(b):
                act.dma_start(nat_int, one(mask_t, b)).then_inc(mask_loaded, 16)

            def load_gate(b):
                act.dma_start(nat[:, :, :], one(gate_t, b)).then_inc(gate_loaded, 16)

            def load_ctx(b):
                c = ctx[b] if isinstance(b, int) else ctx[bass.ds(b, 1)].rearrange("b k d -> (b k) d")
                act.dma_start(ctx_nat[:, 0:KT - 1, :], c[0:(KT - 1) * P, :].rearrange("(t p) d -> p t d", p=P))\
                   .then_inc(ctx_loaded, 16)
                act.dma_start(ctx_nat[0:REST, KT - 1, :], c[(KT - 1) * P:SK, :]).then_inc(ctx_loaded, 16)

            def load_x1(b, u):
                act.dma_start(x1_nat[u][:, :, :], one(x1_t, b)).then_inc(x1_loaded[u], 16)

            def mine(name):
                return name[0] in "fk" or name in ("x1", "q", "row") or name[:3] == "ctx"

            def copy_job(J, name):
                k = int(name[-1]) if name[-1].isdigit() else 0
                act.wait_ge(misc_ready, J + 1)
                if name[0] == "f" and k < 6:
                    act.activation(gate_T[:, 2 * k:2 * k + 2, :].rearrange("p t q -> p (t q)"), ps_misc[:, :],
                                   ACT.Copy).then_inc(misc_read, 1)
                elif name == "f6":
                    act.activation(gate_T[0:REST, KT - 1, :], ps_misc[0:REST, 0:SQ], ACT.Copy).then_inc(misc_read, 1)
                elif name[:3] == "ctx":
                    n = 4 * P if k < 3 else REST
                    act.activation(ctx_T[:, 4 * P * k:4 * P * k + n], ps_misc[:, 0:n], ACT.Copy).then_inc(misc_read, 1)
                elif name == "x1":
                    act.activation(x1_T[:, :], ps_misc[:, 0:SQ], ACT.Copy).then_inc(misc_read, 1)
                elif name[0] == "k":
                    n = PK // 4
                    act.activation(k_f[:, n * k:n * k + n], ps_misc[:, 0:n], ACT.Identity, bias=b_qk[:, 1:2])\
                       .then_inc(misc_read, 1)
                elif name == "q":
                    act.activation(q_f[:, :], ps_misc[:, 0:SQ], ACT.Identity, bias=b_qk[:, 0:1], scale=SCALE)\
                       .then_inc(misc_read, 1)
                elif name == "row":
                    act.activation(row_bf[:, :], ps_misc[0:KT, 0:P], ACT.Copy).then_inc(misc_read, 1)

            def part(b, n, copied):
                if n:
                    act.wait_ge(rest_made[n - 1], b + 1)
                else:
                    act.wait_ge(misc_read, copied)
                    if not (isinstance(b, int) and b == 0):
                        for g in range(G):
                            act.wait_ge(k_loaded[g], b * (13 * 16))
                act.activation(q_part[n][:, :], q_f[:, :], ACT.Copy)
                act.activation(k_part[n][:, :], k_f, ACT.Copy).then_inc(part_made[n], 1)

            def fill(b, u):
                act.wait_ge(mask_loaded, b * 16 + 16)
                for t in range(QT):
                    last = act.activation(neg[u][:, t, 0:SK], nat_int[:, t, :], ACT.Copy, scale=-NEG, bias=NEG)
                last.then_inc(neg_made, 1)
                act.wait_ge(neg_made, b + 1)
                load_gate(b)

            def copy_sums(c, n):
                act.wait_ge(applied, n + (1 - LAG + RING))
                act.wait_ge(o_normed, c)
                act.activation(o_sb[:, :], ps_o[:, :], ACT.Copy).then_inc(o_copied, 1)

            def store(b):
                act.wait_ge(y2_ready, b + 1)
                act.dma_start(one(y2_t, b), y2[:, :, :]).then_inc(y2_stored, 16)

            def prologue():
                act.sem_inc(exp_ready, 2)
                act.sem_inc(o_copied, 1)
                act.wait_ge(set_dve, N_SET)
                load_ctx(0)
                load_x1(0, 0)
                load_mask(0)
                act.wait_ge(b_ready, 2)
                for J, name in enumerate(PREPARE):
                    if mine(name):
                        copy_job(J, name)
                    if name == "q":
                        part(0, 0, J + 1)
                        fill(0, 0)
                    if name == "row":
                        part(0, 1, 0)
                        part(0, 2, 0)

            def cycle(b, u, jobs, is_first, is_last):
                for g, t, n, todo in walk(jobs, b, is_first):
                    if (g, t) == (0, 0) and not is_last:
                        act.wait_ge(part_made[2], b + 1)
                        load_ctx(b + 1)
                    if t == LAG and not (is_first and g == 0):
                        copy_sums(b * G + (g - 1), n - 1)
                    w = weights[(g * KT + t) % RING]
                    act.wait_ge(applied, n + 1)
                    for pair in range(2):
                        act.wait_ge(s_ready, n * 2 + (pair + 1))
                        act.activation(w[:, 2 * pair:2 * pair + 2, SQ:], ps_s[pair][:, :].rearrange("p (h q) -> p h q", h=2),
                                       ACT.Exp).then_inc(exp_ready, 1)
                    for J, name in todo:
                        if name in ("f0", "f1", "f2", "f3", "f4"):
                            upto = 2 * int(name[1]) + 1
                            mine_dve = sum(x <= upto for x in C.DVE_TILES)
                            act.wait_ge(gated_dve, b * (G * N_DVE) + (3 * N_DVE + mine_dve))
                            act.wait_ge(gated_pool, b * (G * N_POOL) + (3 * N_POOL + upto + 1 - mine_dve))
                        if name in ("f5", "f6"):
                            act.wait_ge(gated_dve, b * (G * N_DVE))
                            act.wait_ge(gated_pool, b * (G * N_POOL))
                        if mine(name):
                            copy_job(J, name)
                        if name == "q":
                            part(b + 1, 0, J + 1)
                    if (g, t) == (0, 3) and not is_last:
                        load_mask(b + 1)
                    if (g, t) == (0, 10):
                        if not is_first:
                            store(b - 1)
                        if not is_last:
                            load_x1(b + 1, 1 - u)
                    if not is_last and (g, t) == (1, 10):
                        part(b + 1, 1, 0)
                    if not is_last and (g, t) == (1, 12):
                        fill(b + 1, 1 - u)
                    if not is_last and (g, t) == (2, 3):
                        part(b + 1, 2, 0)

            def epilogue():
                copy_sums(B * G - 1, B * SLOTS - 1 + LAG)
                store(B - 1)
                act.wait_ge(y2_stored, 16 * B)

            cycles(act, prologue, cycle, epilogue)

        @block.vector
        def _(dve):
            def unit(b, g, u, k):
                h, qt, half = k // (2 * QT), k // 2 % QT, k % 2
                m = b * (G * UNITS) + (g * UNITS + k)
                lo, n = half * HALF[0], HALF[half]
                if k == 0:
                    dve.wait_ge(neg_made, b + 1)
                dve.wait_ge(m_ready, m + 1)
                pass_wait(dve, passed)
                dve.tensor_tensor_reduce(out=swept[k % 2][:, 0:n], in0=ps_m[k % 2][:, 0:n], in1=neg[u][:, qt, lo:lo + n],
                                         scale=1.0, scalar=-3.0e38, op0=ALU.add, op1=ALU.max,
                                         accum_out=top2[:, h * QT + qt, half:half + 1]).then_inc(m_read, 1)

            def join(b, g):
                dve.wait_ge(m_read, b * (G * UNITS) + ((g + 1) * UNITS + 2))
                dve.tensor_tensor(top[:, :], top2[:, :, 0], top2[:, :, 1], ALU.max).then_inc(top_ready, 1)

            def split(J, b, g):
                x = ps_misc[0:HG * QT, 0:P]
                c = b * G + g
                dve.wait_ge(misc_ready, J + 1)
                dve.tensor_scalar(top_part[0][:, :], x, -1.0, None, ALU.mult).then_inc(top_step, 1)
                dve.wait_ge(top_step, c * 2 + 1)
                dve.scalar_tensor_tensor(out=top_r[:, :], in0=x, scalar=-1.0, in1=top_part[0][:, :],
                                         op0=ALU.mult, op1=ALU.subtract).then_inc(misc_read, 1)
                dve.wait_ge(misc_read, J + 1)
                dve.tensor_copy(top_part[1][:, :], top_r[:, :]).then_inc(top_step, 1)
                dve.wait_ge(top_step, c * 2 + 2)
                dve.tensor_tensor(top_part[2][:, :], top_r[:, :], top_part[1][:, :], ALU.subtract).then_inc(top_split, 1)

            def count(J, b):
                dve.wait_ge(misc_ready, J + 1)
                dve.tensor_scalar(seen[:, 0, :], ps_misc[:, 0:KT], 0.0, None, ALU.is_equal)
                dve.tensor_scalar(seen[:, 1, :], ps_misc[:, 0:KT], SQ * NEG, None, ALU.is_le).then_inc(misc_read, 1)
                dve.wait_ge(misc_read, J + 1)
                dve.tensor_reduce(seen_n[:, :], seen[:, :, :], AX_X, ALU.add).then_inc(seen_ready, 1)

            def total(J, b, u):
                dve.wait_ge(misc_ready, J + 1)
                dve.tensor_reduce(whole[:, 0:1], ps_misc[:, 0:2], AX_X, ALU.add)
                dve.tensor_scalar(whole[:, 1:2], ps_misc[:, 0:1], 1.0, None, ALU.is_ge).then_inc(misc_read, 1)
                dve.wait_ge(misc_read, J + 1)
                dve.scalar_tensor_tensor(out=fast[:, :], in0=whole[:, 0:1], scalar=float(PK), in1=whole[:, 1:2],
                                         op0=ALU.is_ge, op1=ALU.mult).then_inc(fast_ready, 1)
                dve.wait_ge(fast_ready, b + 1)
                dve.tensor_scalar(row_c[:, :], seen[:, 1, :], fast[:, 0:1], NEG, ALU.mult, ALU.mult).then_inc(row_ready, 1)
                dve.tensor_scalar(general[u][:, :], fast[:, :], -1.0, 1.0, ALU.mult, ALU.add).then_inc(general_made, 1)

            def add_bias(J, k, u):
                n = 4 if k < KT // 4 else KT % 4
                dve.wait_ge(misc_ready, J + 1)
                dve.tensor_tensor(values[u][:, 4 * k:4 * k + n, 0:H * (DH + 1)].rearrange("p t (h e) -> p t h e", h=H)[:, :, :, 0:DH],
                                  ps_misc[:, 0:n * P].rearrange("p (t h d) -> p t h d", t=n, h=H),
                                  bv_sb[:, :].rearrange("p (h d) -> p h d", h=H).unsqueeze(1).to_broadcast([P, n, H, DH]),
                                  ALU.add).then_inc(misc_read, 1)

            def normalize(J, g):
                dve.wait_ge(misc_ready, J + 1)
                dve.reciprocal(inv[:, :], ps_misc[:, 0:SQ]).then_inc(misc_read, 1)
                dve.wait_ge(misc_read, J + 1)
                dve.tensor_tensor(o_T[:, g, :], o_sb[:, 0:SQ], inv[:, :], ALU.mult).then_inc(o_normed, 1)

            def residual(J, b, u):
                dve.wait_ge(misc_ready, J + 1)
                dve.wait_ge(y2_stored, b * 16)
                dve.tensor_tensor(y2[:, :, :], ps_misc[:, 0:QT * D].rearrange("p (t d) -> p t d", t=QT),
                                  bo_sb[:, :].unsqueeze(1).to_broadcast([P, QT, D]), ALU.add).then_inc(misc_read, 1)
                dve.wait_ge(misc_read, J + 1)
                dve.tensor_tensor(y2[:, :, :], y2[:, :, :], x1_nat[u][:, :, :], ALU.add).then_inc(y2_ready, 1)

            def prologue():
                dve.wait_ge(w_loaded, 16 * (7 + HG))
                for n in range(2):
                    dve.tensor_copy(b_perm[:, n, :].rearrange("p (g d a) -> p g a d", g=G, d=DH),
                                    b_rows[:, n, :].rearrange("p (g a d) -> p g a d", g=G, a=HG)).then_inc(set_dve, 1)
                for n in range(2):
                    dve.tensor_copy(w_sb[:, n, :].rearrange("p (g d a) -> p g a d", g=G, d=DH),
                                    w_nat[:, n, :].rearrange("p (g a d) -> p g a d", g=G, a=HG)).then_inc(set_dve, 1)
                dve.memset(ctx_T[:, SK:PK], 0.0).then_inc(set_dve, 1)
                dve.memset(gate_T[:, KT - 1, :], 0.0).then_inc(set_dve, 1)
                for u in range(2):
                    dve.memset(q_aug[u][64:TOP, :, :], 1.0).then_inc(set_dve, 1)
                for u in range(2):
                    dve.memset(neg[u][:, :, SK:PK], 4 * NEG)
                    dve.memset(values[u][:, :, :], 1.0).then_inc(set_dve, 1)
                dve.sem_inc(m_read, 2)
                dve.wait_ge(b_turned, 1)
                dve.tensor_scalar(b_qk[:, 0:1], ps_misc[:, 0:1], SCALE, None, ALU.mult).then_inc(b_ready, 1)
                dve.tensor_copy(b_qk[:, 1:2], ps_misc[:, 1:2]).then_inc(b_ready, 1)
                for J, name in enumerate(PREPARE):
                    if name[0] == "v":
                        add_bias(J, int(name[1]), 0)
                    if name == "count":
                        count(J, 0)
                    if name == "total":
                        total(J, 0, 0)
                    if name == "top":
                        for k in range(UNITS):
                            unit(0, 0, 0, k)
                        join(0, 0)
                        split(J, 0, 0)

            def cycle(b, u, jobs, is_first, is_last):
                for g, t, n, todo in walk(jobs, b, is_first):
                    ahead = (b, g + 1, u) if g < G - 1 else (b + 1, 0, 1 - u)
                    if t < 8 and not (is_last and g == G - 1):
                        unit(*ahead, 2 * t)
                        unit(*ahead, 2 * t + 1)
                    if t == 8 and not (is_last and g == G - 1):
                        join(*ahead[:2])
                    if t in C.DVE_TILES:
                        dve.wait_ge(exp_ready, n * 2 + 4)
                        w = weights[(g * KT + t) % RING]
                        dve.tensor_tensor(w[:, :, 0:SQ], w[:, :, SQ:],
                                          gate_T[:, t, :].unsqueeze(1).to_broadcast([P, HG, SQ]), ALU.mult)\
                           .then_inc(gated_dve, 1)
                    for J, name in todo:
                        if name[0] == "v":
                            add_bias(J, int(name[1]), 1 - u)
                        if name == "count":
                            count(J, b + 1)
                        if name == "total":
                            total(J, b + 1, 1 - u)
                        if name == "top":
                            split(J, *ahead[:2])
                        if name[:3] == "den":
                            normalize(J, int(name[3]))
                        if name == "out":
                            residual(J, b - 1, 1 - u)

            def epilogue():
                normalize(END_JOB, G - 1)
                residual(END_JOB + 1, B - 1, (B - 1) % 2)

            cycles(dve, prologue, cycle, epilogue)

        @block.tensor
        def _(pe):
            def unit(b, g, u, k):
                h, qt, half = HG * g + k // (2 * QT), k // 2 % QT, k % 2
                m = b * (G * UNITS) + (g * UNITS + k)
                lo, n = half * HALF[0], HALF[half]
                if k == 0:
                    pe.wait_ge(k_loaded[g], b * (13 * 16) + 13 * 16)
                    pe.wait_ge(q_loaded[u], b * (18 * 16) + (2 - u) * (18 * 16))
                pe.wait_ge(m_read, m + 1)
                for x in (0, 512):
                    last = pe.matmul(ps_m[k % 2][:, x:min(x + 512, n)], q_aug[u][0:TOP, h, qt * P:(qt + 1) * P],
                                     k_aug[0:TOP, h, lo + x:lo + min(x + 512, n)], start=True, stop=True)
                last.then_inc(m_ready, 1)

            def scores(b, g, t, n, u, general_way):
                tile = slice(t * P, (t + 1) * P)
                if t == 0:
                    pe.wait_ge(top_loaded[g % 2], b * 96 + 48 * (g // 2 + 1))
                for pair in range(2):
                    pe.wait_ge(exp_ready, n * 2 + (pair + 1))
                    for j in range(2):
                        h = HG * g + 2 * pair + j
                        dst = ps_s[pair][:, j * SQ:(j + 1) * SQ]
                        if not general_way:
                            last = pe.matmul(dst, k_aug[0:TOP + 3, h, tile], q_aug[u][0:TOP + 3, h, :], start=True, stop=True)
                            continue
                        pe.matmul(dst, k_aug[0:TOP, h, tile], q_aug[u][0:TOP, h, :], start=True, stop=False)
                        for qt in range(QT):
                            pe.matmul(dst[:, qt * P:(qt + 1) * P], neg[u][:, qt, tile], ident_bf[:, :], start=False, stop=False)
                        last = pe.matmul(dst, k_aug[TOP:TOP + 3, h, tile], q_aug[u][TOP:TOP + 3, h, :], start=False, stop=True)
                    last.then_inc(s_ready, 1)

            def apply(c, g, t, n, u):
                mine_dve = sum(x <= t for x in C.DVE_TILES)
                pe.wait_ge(exp_ready, n * 2 + 4)
                if t in C.DVE_TILES:
                    pe.wait_ge(gated_dve, c * N_DVE + mine_dve)
                else:
                    pe.wait_ge(gated_pool, c * N_POOL + (t + 1 - mine_dve))
                if t == 0:
                    pe.wait_ge(o_copied, c + 1)
                for j in range(HG):
                    h = HG * g + j
                    last = pe.matmul(ps_o[32 * j:32 * j + 32, :], values[u][:, t, (DH + 1) * h:(DH + 1) * h + 32],
                                     weights[(g * KT + t) % RING][:, j, :], start=(t == 0), stop=(t == KT - 1))
                last.then_inc(applied, 1)

            def job(J, name, b, u, c=None):
                k = int(name[-1]) if name[-1].isdigit() else 0
                if name in ("f0", "f5"):
                    pe.wait_ge(gate_loaded, b * 16 + 16)
                if name == "ctx0":
                    pe.wait_ge(ctx_loaded, b * 32 + 32)
                if name == "x1":
                    pe.wait_ge(x1_loaded[u], b * 8 + (16 - 8 * u))
                if name == "count":
                    pe.wait_ge(neg_made, b + 1)
                if name == "total":
                    pe.wait_ge(seen_ready, b + 1)
                if name == "row":
                    pe.wait_ge(row_ready, b + 1)
                if name == "top":
                    pe.wait_ge(top_ready, c + 1)
                if name[:3] == "den":
                    pe.wait_ge(o_copied, c + 2)
                if name == "out":
                    pe.wait_ge(o_normed, c + 1)
                pe.wait_ge(misc_read, J)
                if name[0] == "f":
                    for j in range(2 if k < 6 else 1):
                        for qt in range(QT):
                            w = P if k < 6 else REST
                            at = (QT * j + qt) * P
                            last = pe.transpose(ps_misc[0:w, at:at + P], nat[:, qt, (2 * k + j) * P:(2 * k + j) * P + w], ident[:, :])
                elif name[:3] == "ctx":
                    for j in range(4 if k < 3 else 1):
                        w = P if k < 3 else REST
                        last = pe.transpose(ps_misc[:, j * P:j * P + w], ctx_nat[0:w, 4 * k + j, :], ident[0:w, 0:w])
                elif name == "x1":
                    for qt in range(QT):
                        last = pe.transpose(ps_misc[:, qt * P:(qt + 1) * P], x1_nat[u][:, qt, :], ident[:, :])
                elif name[0] == "k":
                    n = PK // 4
                    last = pe.matmul(ps_misc[:, 0:n], w_sb[:, 1, :], ctx_T[:, n * k:n * k + n], start=True, stop=True)
                elif name == "q":
                    last = pe.matmul(ps_misc[:, 0:SQ], w_sb[:, 0, :], x1_T[:, :], start=True, stop=True)
                elif name[0] == "v":
                    for j in range(4 if k < KT // 4 else KT % 4):
                        last = pe.matmul(ps_misc[:, j * P:(j + 1) * P], ctx_T[:, (4 * k + j) * P:(4 * k + j + 1) * P], wv_sb[:, :],
                                         start=True, stop=True)
                elif name == "count":
                    for t in range(KT):
                        for qt in range(QT):
                            last = pe.matmul(ps_misc[:, t:t + 1], neg[u][:, qt, t * P:(t + 1) * P], ones_bf[:, :],
                                             start=(qt == 0), stop=(qt == QT - 1))
                elif name == "total":
                    last = pe.matmul(ps_misc[:, 0:2], ones[:, :], seen_n[:, :], start=True, stop=True)
                elif name == "row":
                    last = pe.transpose(ps_misc[0:KT, 0:P], row_c[:, :], ident[:, :])
                elif name == "top":
                    last = pe.transpose(ps_misc[0:HG * QT, 0:P], top[:, :], ident[:, :])
                elif name[:3] == "den":
                    last = pe.matmul(ps_misc[:, 0:SQ], spread[:, :], o_sb[:, SQ:], start=True, stop=True)
                elif name == "out":
                    for qt in range(QT):
                        for g in range(G):
                            last = pe.matmul(ps_misc[:, qt * D:(qt + 1) * D], o_T[:, g, qt * P:(qt + 1) * P], wo_sb[:, g, :],
                                             start=(g == 0), stop=(g == G - 1))
                last.then_inc(misc_ready, 1)

            def prologue():
                pe.sem_inc(applied, RING)
                pe.wait_ge(made, 8)
                pe.wait_ge(w_loaded, 16 * (7 + HG))
                pe.wait_ge(set_dve, N_SET)
                for n in range(2):
                    last = pe.matmul(ps_misc[:, n:n + 1], b_perm[:, n, :], ones[0:1, 0:1], start=True, stop=True)
                last.then_inc(b_turned, 1)
                pe.wait_ge(b_ready, 2)
                for J, name in enumerate(PREPARE):
                    if name == "top":
                        for k in range(UNITS):
                            unit(0, 0, 0, k)
                    job(J, name, 0, 0, 0)

            def outline(b, u, jobs, is_first, is_last, general_way):
                for g, t, n, todo in walk(jobs, b, is_first):
                    ahead = (b, g + 1, u) if g < G - 1 else (b + 1, 0, 1 - u)
                    scores(b, g, t, n, u, general_way)
                    if t < 8 and not (is_last and g == G - 1):
                        unit(*ahead, 2 * t)
                        unit(*ahead, 2 * t + 1)
                    for J, name in todo:
                        if name in ("f5", "f6"):
                            job(J, name, b, u)
                        elif name == "top":
                            job(J, name, None, None, b * G + (g + 1))
                        elif name[:3] == "den":
                            job(J, name, None, None, b * G + (g - 1))
                        elif name == "out":
                            job(J, name, None, None, b * G - 1)
                        else:
                            job(J, name, b + 1, 1 - u)
                    back = g * KT + t - LAG
                    if back >= 0:
                        apply(b * G + back // KT, back // KT, back % KT, n - LAG, u)
                    elif not is_first:
                        apply(b * G - 1, G - 1, KT + back, n - LAG, 1 - u)

            def cycle(b, u, jobs, is_first, is_last):
                pe.wait_ge(general_made, b + 1)
                pass_wait(pe, passed)
                any_mask = pe.value_load(general[u][0:1, 0:1])
                with pe.If_eq(pe.to_reg(any_mask), 0):
                    outline(b, u, jobs, is_first, is_last, False)
                with pe.Else():
                    outline(b, u, jobs, is_first, is_last, True)

            def epilogue():
                for back in range(LAG):
                    apply(B * G - 1, G - 1, KT - LAG + back, B * SLOTS - LAG + back, (B - 1) % 2)
                job(END_JOB, "den3", None, None, B * G - 1)
                job(END_JOB + 1, "out", None, None, B * G - 1)

            cycles(pe, prologue, cycle, epilogue)


def experts_pass(nc, y2_dram, router_W, router_b, sW1, sb1, sW2, sb2, eW1, eb1, eW2, eb2, out):
    E, D, H = eW1.shape
    K = 3
    chunks = y2_dram.shape[0] // CH
    JOBS = E + 1
    y2_t = y2_dram.rearrange("(c t p) d -> c p t d", t=TT, p=P)
    out_t = out.rearrange("b l d -> (b l) d").rearrange("(c t p) d -> c p t d", t=TT, p=P)

    with Scope(nc, "moe") as s:
        ident = s.sb("ident", [P, P])
        earlier = s.sb("earlier", [P, E, E])
        w1 = s.sb("w1", [P, JOBS, H])
        w2 = s.sb("w2", [P, JOBS, D])
        b1_rows = s.sb("b1_rows", [JOBS, H])
        b1 = s.sb("b1", [P, JOBS])
        b2 = s.sb("b2", [E, D])
        b2_shared = s.sb("b2_shared", [P, D])
        w_router = s.sb("w_router", [P, E])
        b_router = s.sb("b_router", [P, E])
        eps = s.sb("eps", [P, 1])
        yin = [s.sb(f"yin{u}", [P, TT, D]) for u in range(2)]
        x2 = s.sb("x2", [P, TT, D])
        acc = [s.sb(f"acc{u}", [P, TT, D]) for u in range(2)]
        x2T = [s.sb(f"x2T{u}", [P, CH]) for u in range(2)]
        cw = [s.sb(f"cw{u}", [P, TT, E]) for u in range(2)]
        cwT = [s.sb(f"cwT{u}", [E, CH]) for u in range(2)]
        hT = [s.sb(f"hT{u}", [P, CH]) for u in range(2)]
        res = [s.sb(f"res{u}", [P, TT, D]) for u in range(2)]
        stats = s.sb("stats", [P, TT, 6])
        mv = s.sb("mv", [P, TT, 2])
        std = s.sb("std", [P, TT])
        rstd = s.sb("rstd", [P, TT])
        logit = s.sb("logit", [P, TT, E])
        peak = s.sb("peak", [P, TT])
        shifted = s.sb("shifted", [P, TT, E])
        expd = s.sb("expd", [P, TT, E])
        total = s.sb("total", [P, TT])
        inv_total = s.sb("inv_total", [P, TT])
        prob = s.sb("prob", [P, TT, E])
        above = s.sb("above", [P, TT, E, E])
        tied = s.sb("tied", [P, TT, E, E])
        rank = s.sb("rank", [P, TT, E])
        ps_x = s.ps("ps_x", [P, CH])
        ps_r = s.ps("ps_r", [P, 512])
        ps_h = [s.ps(f"ps_h{u}", [P, CH]) for u in range(2)]
        ps_y = [s.ps(f"ps_y{u}", [P, CH]) for u in range(2)]
        ps_acc = s.ps("ps_acc", [P, CH])

        w_loaded, y_loaded = s.sem("w_loaded"), [s.sem(f"y_loaded{u}") for u in range(2)]
        zeroed, ident_made, set_up = s.sem("zeroed"), s.sem("ident_made"), s.sem("set_up")
        passed = s.sem("passed")
        b1_ready, b1_copied = s.sem("b1_ready"), s.sem("b1_copied")
        yin_free = s.sem("yin_free")
        step = s.sem("step")
        var_ready, std_ready, x2_ready = s.sem("var_ready"), s.sem("std_ready"), s.sem("x2_ready")
        x2T_ready, x2T_copied = s.sem("x2T_ready"), s.sem("x2T_copied")
        router_ready, shifted_ready, exp_ready = s.sem("router_ready"), s.sem("shifted_ready"), s.sem("exp_ready")
        cw_ready, cwT_ready, cwT_copied = s.sem("cw_ready"), s.sem("cwT_ready"), s.sem("cwT_copied")
        h_ready = s.sem("h_ready")
        h_copied = s.sem("h_copied")
        o_ready = s.sem("o_ready")
        o_read = s.sem("o_read")
        var2_ready, std2_ready = s.sem("var2_ready"), s.sem("std2_ready")
        above_ready, rank_ready = s.sem("above_ready"), s.sem("rank_ready")
        res_ready, res_free = s.sem("res_ready"), s.sem("res_free")
        stored = [s.sem(f"stored{u}") for u in range(2)]
        block = s.stack.enter_context(nc.Block())
        loads = [(w1[:, 0:E, :], eW1.rearrange("e d h -> d e h")), (w1[:, E, :], sW1),
                 (w2[:, 0:E, :], eW2.rearrange("e h d -> h e d")), (w2[:, E, :], sW2),
                 (b1_rows[0:E, :], eb1), (b1_rows[E:JOBS, :], sb1.rearrange("(a h) -> a h", a=1)),
                 (b2[:, :], eb2), (b2_shared[:, :], row_bcast(sb2)), (w_router[:, :], router_W),
                 (b_router[:, :], row_bcast(router_b))]
        n_w = 16 * len(loads)
        PAIRS = chunks // 2 - 1

        @block.sync
        def _(sp):
            for dst, src in loads[4:] + loads[:4]:
                sp.dma_start(dst, src).then_inc(w_loaded, 16)
            with sp.Fori(0, chunks // 2) as i:
                for u in range(2):
                    c = i * 2 + u
                    sp.wait_ge(yin_free, c + 1)
                    sp.dma_start(yin[u][:, :, :], y2_t[bass.ds(c, 1)].rearrange("c p t d -> (c p) t d")).then_inc(y_loaded[u], 16)

        @block.gpsimd
        def _(pool):
            make_identity(pool, ident, zeroed, ident_made)
            pool.memset(eps[:, :], EPS).then_inc(set_up, 1)
            pool.memset(earlier[:, :, :], 1.0).then_inc(set_up, 1)
            pool.wait_ge(set_up, 2)
            pool.affine_select(out=earlier[:, :, :], in_=earlier[:, :, :], compare_op=ALU.is_gt, fill=0.0,
                               base=0, pattern=[[1, E], [-1, E]], channel_multiplier=0).then_inc(set_up, 1)
            pool.sem_inc(res_free, 2)
            with pool.Fori(0, chunks // 2) as i:
                for u in range(2):
                    c = i * 2 + u
                    pool.wait_ge(res_ready, c + 1)
                    pool.dma_start(out_t[bass.ds(c, 1)].rearrange("c p t d -> (c p) t d"), res[u][:, :, :]).then_inc(stored[u], 16)
                    pool.wait_ge(stored[u], i * 16 + 16)
                    pool.sem_inc(res_free, 1)

        @block.tensor
        def _(pe):
            def hidden(n, e, u):
                pe.wait_ge(h_copied, n + 1)
                pe.matmul(ps_h[e % 2][:, :], w1[:, e, :], x2T[u][:, :], start=True, stop=True).then_inc(h_ready, 1)

            def second(n, e, u):
                pe.wait_ge(h_copied, n + 3)
                pe.wait_ge(o_read, n + 1)
                dst = ps_y[e % 2] if e < E else ps_acc
                for t in range(TT):
                    tile = slice(t * P, (t + 1) * P)
                    last = pe.matmul(dst[:, tile], hT[e % 2][:, tile], w2[:, e, :], start=True, stop=e < E)
                    if e == E:
                        last = pe.matmul(dst[:, tile], cwT[u][:, tile], b2[:, :], start=False, stop=True)
                last.then_inc(o_ready, 1)

            def turn_x2(c, u):
                pe.wait_ge(x2_ready, c + 1)
                for t in range(TT):
                    last = pe.transpose(ps_x[:, t * P:(t + 1) * P], x2[:, t, :], ident[:, :])
                last.then_inc(x2T_ready, 1)

            def route(c, u):
                pe.wait_ge(x2T_copied, c + 1)
                for t in range(TT):
                    last = pe.matmul(ps_r[:, t * E:(t + 1) * E], x2T[u][:, t * P:(t + 1) * P], w_router[:, :],
                                     start=True, stop=True)
                last.then_inc(router_ready, 1)

            def turn_cw(c, u):
                pe.wait_ge(cw_ready, c + 1)
                for t in range(TT):
                    last = pe.transpose(ps_x[0:E, t * P:(t + 1) * P], cw[u][:, t, :], ident[:, :])
                last.then_inc(cwT_ready, 1)

            def chunk(c, u, prepare):
                hidden(c * JOBS, 0, u)
                for e in range(JOBS):
                    if e + 1 < JOBS:
                        hidden(c * JOBS + (e + 1), e + 1, u)
                    if e == E:
                        pe.wait_ge(cwT_copied, c + 1)
                    second(c * JOBS + e, e, u)
                    if prepare and e == 5:
                        turn_x2(c + 1, 1 - u)
                    if prepare and e == 7:
                        route(c + 1, 1 - u)
                    if prepare and e == 13:
                        turn_cw(c + 1, 1 - u)

            pe.wait_ge(w_loaded, n_w)
            pe.wait_ge(ident_made, 1)
            pe.transpose(ps_x[:, 0:JOBS], b1_rows[:, :], ident[0:JOBS, 0:JOBS]).then_inc(b1_ready, 1)
            pe.wait_ge(b1_copied, 1)
            turn_x2(0, 0)
            route(0, 0)
            turn_cw(0, 0)
            with pe.Fori(0, PAIRS) as i:
                for u in range(2):
                    chunk(i * 2 + u, u, True)
            chunk(chunks - 2, 0, True)
            chunk(chunks - 1, 1, False)

        @block.scalar
        def _(act):
            def relu(n, e):
                act.wait_ge(h_ready, n + 1)
                act.wait_ge(o_ready, n + 1)
                act.activation(hT[e % 2][:, :], ps_h[e % 2][:, :], ACT.Relu, bias=b1[:, e:e + 1]).then_inc(h_copied, 1)

            def root_x2(c):
                act.wait_ge(var_ready, c + 1)
                act.activation(std[:, :], mv[:, :, 1], ACT.Sqrt, bias=eps[:, :]).then_inc(std_ready, 1)

            def copy_x2T(c, u):
                act.wait_ge(x2T_ready, c + 1)
                act.activation(x2T[u][:, :], ps_x[:, :], ACT.Copy).then_inc(x2T_copied, 1)

            def exponent(c):
                act.wait_ge(shifted_ready, c + 1)
                act.activation(expd[:, :, :], shifted[:, :, :], ACT.Exp).then_inc(exp_ready, 1)

            def copy_cwT(c, u):
                act.wait_ge(cwT_ready, c + 1)
                act.activation(cwT[u][:, :], ps_x[0:E, :], ACT.Copy).then_inc(cwT_copied, 1)

            def chunk(c, u, prepare):
                for e in range(JOBS):
                    relu(c * JOBS + e, e)
                    if prepare and e == 2:
                        root_x2(c + 1)
                    if prepare and e == 6:
                        copy_x2T(c + 1, 1 - u)
                    if prepare and e == 10:
                        exponent(c + 1)
                    if prepare and e == 14:
                        copy_cwT(c + 1, 1 - u)
                act.wait_ge(var2_ready, c + 1)
                act.activation(std[:, :], mv[:, :, 1], ACT.Sqrt, bias=eps[:, :]).then_inc(std2_ready, 1)

            act.wait_ge(b1_ready, 1)
            act.activation(b1[:, :], ps_x[:, 0:JOBS], ACT.Copy).then_inc(b1_copied, 1)
            act.sem_inc(h_copied, 2)
            act.sem_inc(o_ready, 2)
            act.wait_ge(set_up, 3)
            act.wait_ge(b1_copied, 1)
            root_x2(0)
            copy_x2T(0, 0)
            exponent(0)
            copy_cwT(0, 0)
            with act.Fori(0, PAIRS) as i:
                for u in range(2):
                    chunk(i * 2 + u, u, True)
            chunk(chunks - 2, 0, True)
            chunk(chunks - 1, 1, False)

        @block.vector
        def _(dve):
            PREP, FIN = 11, 2
            per = PREP + FIN

            def over(ap, n):
                return ap.unsqueeze(2).to_broadcast([P, TT, n])

            def variance(c, u, base):
                dve.wait_ge(y_loaded[u], ((c - u) * 8 + 16) if not isinstance(c, int) else 16 * (c // 2 + 1))
                for t in range(TT):
                    last = dve.bn_stats(stats[:, t, :], yin[u][:, t, :])
                last.then_inc(step, 1)
                dve.wait_ge(step, base + 1)
                pass_wait(dve, passed)
                for t in range(TT):
                    last = dve.bn_aggr(mv[:, t, :], stats[:, t, :])
                last.then_inc(var_ready, 1)

            def normalize(c, u, base):
                dve.wait_ge(std_ready, c + 1)
                dve.reciprocal(rstd[:, :], std[:, :]).then_inc(step, 1)
                dve.wait_ge(step, base + 2)
                for t in range(TT):
                    last = dve.tensor_scalar(x2[:, t, :], yin[u][:, t, :], mv[:, t, 0:1], rstd[:, t:t + 1],
                                             ALU.subtract, ALU.mult)
                last.then_inc(x2_ready, 1)
                dve.wait_ge(x2_ready, c + 1)
                dve.tensor_tensor(acc[u][:, :, :], x2[:, :, :], b2_shared[:, :].unsqueeze(1).to_broadcast([P, TT, D]),
                                  ALU.add).then_inc(step, 1)
                dve.sem_inc(yin_free, 1)

            def shift(c, base):
                dve.wait_ge(router_ready, c + 1)
                dve.tensor_tensor(logit[:, :, :], ps_r[:, 0:TT * E].rearrange("p (t e) -> p t e", t=TT),
                                  b_router[:, :].unsqueeze(1).to_broadcast([P, TT, E]), ALU.add).then_inc(step, 1)
                dve.wait_ge(step, base + 4)
                dve.tensor_reduce(peak[:, :], logit[:, :, :], AX_X, ALU.max).then_inc(step, 1)
                dve.wait_ge(step, base + 5)
                dve.tensor_tensor(shifted[:, :, :], logit[:, :, :], over(peak[:, :], E), ALU.subtract).then_inc(shifted_ready, 1)

            def weigh(c, u, base):
                dve.wait_ge(exp_ready, c + 1)
                dve.tensor_reduce(total[:, :], expd[:, :, :], AX_X, ALU.add).then_inc(step, 1)
                dve.wait_ge(step, base + 6)
                dve.reciprocal(inv_total[:, :], total[:, :]).then_inc(step, 1)
                dve.wait_ge(step, base + 7)
                dve.tensor_tensor(prob[:, :, :], expd[:, :, :], over(inv_total[:, :], E), ALU.mult).then_inc(step, 1)
                dve.wait_ge(step, base + 8)
                other = prob[:, :, :].unsqueeze(2).to_broadcast([P, TT, E, E])
                own = prob[:, :, :].unsqueeze(3).to_broadcast([P, TT, E, E])
                dve.tensor_tensor(tied[:, :, :, :], other, own, ALU.is_equal).then_inc(step, 1)
                dve.tensor_tensor(above[:, :, :, :], other, own, ALU.is_gt).then_inc(step, 1)
                dve.wait_ge(step, base + 9)
                for t in range(TT):
                    last = dve.tensor_tensor(tied[:, t, :, :], tied[:, t, :, :], earlier[:, :, :], ALU.mult)
                last.then_inc(step, 1)
                dve.wait_ge(step, base + 11)
                dve.tensor_tensor(above[:, :, :, :], above[:, :, :, :], tied[:, :, :, :], ALU.add).then_inc(above_ready, 1)
                dve.wait_ge(above_ready, c + 1)
                dve.tensor_reduce(rank[:, :, :], above[:, :, :, :], AX_X, ALU.add).then_inc(rank_ready, 1)
                dve.wait_ge(rank_ready, c + 1)
                dve.scalar_tensor_tensor(out=cw[u][:, :, :], in0=rank[:, :, :], scalar=float(K), in1=prob[:, :, :],
                                         op0=ALU.is_lt, op1=ALU.mult).then_inc(cw_ready, 1)

            def chunk(c, u, prepare):
                ahead = c * per + PREP
                dve.wait_ge(cw_ready, c + 1)
                for e in range(E):
                    n = c * JOBS + e
                    dve.wait_ge(o_ready, n + 3)
                    if e:
                        dve.wait_ge(o_read, n + 2)
                    for t in range(TT):
                        last = dve.scalar_tensor_tensor(out=acc[u][:, t, :], in0=ps_y[e % 2][:, t * P:(t + 1) * P],
                                                        scalar=cw[u][:, t, e:e + 1], in1=acc[u][:, t, :],
                                                        op0=ALU.mult, op1=ALU.add)
                    last.then_inc(o_read, 1)
                    if prepare and e == 1:
                        variance(c + 1, 1 - u, ahead)
                    if prepare and e == 3:
                        normalize(c + 1, 1 - u, ahead)
                    if prepare and e == 8:
                        shift(c + 1, ahead)
                    if prepare and e == 10:
                        weigh(c + 1, 1 - u, ahead)
                base = ahead + (PREP if prepare else 0)
                n = c * JOBS + E
                dve.wait_ge(o_ready, n + 3)
                dve.wait_ge(o_read, n + 2)
                dve.tensor_tensor(acc[u][:, :, :], acc[u][:, :, :], ps_acc[:, :].rearrange("p (t d) -> p t d", t=TT),
                                  ALU.add).then_inc(o_read, 1)
                dve.wait_ge(o_read, n + 3)
                for t in range(TT):
                    last = dve.bn_stats(stats[:, t, :], acc[u][:, t, :])
                last.then_inc(step, 1)
                dve.wait_ge(step, base + 1)
                pass_wait(dve, passed)
                for t in range(TT):
                    last = dve.bn_aggr(mv[:, t, :], stats[:, t, :])
                last.then_inc(var2_ready, 1)
                dve.wait_ge(std2_ready, c + 1)
                dve.reciprocal(rstd[:, :], std[:, :]).then_inc(step, 1)
                dve.wait_ge(step, base + 2)
                dve.wait_ge(res_free, c + 1)
                for t in range(TT):
                    last = dve.tensor_scalar(res[u][:, t, :], acc[u][:, t, :], mv[:, t, 0:1], rstd[:, t:t + 1],
                                             ALU.subtract, ALU.mult)
                last.then_inc(res_ready, 1)

            dve.wait_ge(w_loaded, n_w)
            dve.wait_ge(set_up, 3)
            dve.sem_inc(yin_free, 2)
            dve.sem_inc(o_read, 2)
            variance(0, 0, 0)
            normalize(0, 0, 0)
            shift(0, 0)
            weigh(0, 0, 0)
            with dve.Fori(0, PAIRS) as i:
                for u in range(2):
                    chunk(i * 2 + u, u, True)
            chunk(chunks - 2, 0, True)
            chunk(chunks - 1, 1, False)


_INS = ["x", "ctx_1024", "fside_BxSxS2_0", "mask_BxSxS2_ik1"] + ["L0_attn_" + n for n in
        ("W_qkv", "b_qkv", "W_out", "b_out", "weight_q", "weight_v")] + ["L0_xattn_" + n for n in
        ("wq_k", "wq_b", "wk_k", "wk_b", "wv_k", "wv_b", "wo_k", "wo_b")] + ["L0_ffn_" + n for n in
        ("router_W", "router_b", "sW1", "sb1", "sW2", "sb2", "eW1", "eb1", "eW2", "eb2")]


def decoder_layer(nc, a, out, scratch_kind="Internal"):
    B, L, D = a["x"].shape
    x1_dram = nc.dram_tensor("x1_dram", [B * L, D], F32, kind=scratch_kind).ap()
    x2_dram = nc.dram_tensor("x2_dram", [B * L, D], F32, kind=scratch_kind).ap()
    wavelet_pass(nc, a["x"], *[a["L0_attn_" + n] for n in ("W_qkv", "b_qkv", "W_out", "b_out", "weight_q", "weight_v")], x1_dram)
    cross_pass(nc, a["ctx_1024"], a["fside_BxSxS2_0"], a["mask_BxSxS2_ik1"],
               *[a["L0_xattn_" + n] for n in ("wq_k", "wq_b", "wk_k", "wk_b", "wv_k", "wv_b", "wo_k", "wo_b")], x1_dram, x2_dram)
    experts_pass(nc, x2_dram, *[a["L0_ffn_" + n] for n in ("router_W", "router_b", "sW1", "sb1", "sW2", "sb2",
                                                           "eW1", "eb1", "eW2", "eb2")], out)


def kernel(**inputs):
    import numpy as _np
    import concourse.bacc as _bacc
    from concourse import mybir as _mybir
    from concourse.bass_utils import run_bass_kernel_spmd as _run

    nc = _bacc.Bacc("TRN2", target_bir_lowering=False, num_devices=1)
    arrays, args = {}, {}
    for name in _INS:
        a = _np.ascontiguousarray(inputs[name])
        arrays[f"in_{name}_dram"] = a
        args[name] = nc.dram_tensor(f"in_{name}_dram", a.shape, _mybir.dt.from_np(a.dtype), kind="ExternalInput").ap()
    out = nc.dram_tensor("out_0_dram", inputs["x"].shape, _mybir.dt.float32, kind="ExternalOutput").ap()
    decoder_layer(nc, args, out)
    r = _run(nc, [arrays], core_ids=[0])
    return r.results[0]["out_0_dram"]
```

```python
from contextlib import ExitStack

import concourse.bass as bass
from concourse import mybir

F32 = mybir.dt.float32
BF16 = mybir.dt.bfloat16
I32 = mybir.dt.int32
ALU = mybir.AluOpType
ACT = mybir.ActivationFunctionType
AX_X = mybir.AxisListType.X
P = 128
EPS = 1e-5
TT = 4
CH = TT * P


class Scope:

    def __init__(self, nc, name):
        self.nc, self.name, self.stack = nc, name, ExitStack()

    def __enter__(self):
        self.stack.__enter__()
        return self

    def __exit__(self, *a):
        return self.stack.__exit__(*a)

    def sb(self, name, shape, dt=F32):
        return self.stack.enter_context(self.nc.sbuf_tensor(f"{self.name}_{name}", shape, dt))

    def ps(self, name, shape, dt=F32):
        return self.stack.enter_context(self.nc.psum_tensor(f"{self.name}_{name}", shape, dt))

    def sem(self, name):
        return self.stack.enter_context(self.nc.semaphore(f"{self.name}_{name}"))


def pass_wait(eng, passed):
    eng.sem_inc(passed, 1)


def row_bcast(vec, n=P):
    return vec.rearrange("(a m) -> a m", a=1).to_broadcast([n, vec.shape[0]])


def column(vec):
    return vec.rearrange("(m a) -> m a", a=1)


def make_identity(pool, ident, zeroed, made):
    pool.memset(ident[:, :], 0.0).then_inc(zeroed, 1)
    pool.wait_ge(zeroed, 1)
    pool.affine_select(out=ident[:, :], in_=ident[:, :], compare_op=ALU.not_equal, fill=1.0,
                       base=0, pattern=[[-1, P]], channel_multiplier=1).then_inc(made, 1)


def wavelet_pass(nc, x, W_qkv, b_qkv, W_out, b_out, weight_q, weight_v, x1_dram):
    B, L, D = x.shape
    H, M, Dh = weight_q.shape
    chunks = B * L // CH
    S = 0.5 ** 0.5
    x_t = x.rearrange("b l d -> (b l) d").rearrange("(c t p) d -> c p t d", t=TT, p=P)
    x1_t = x1_dram.rearrange("(c t p) d -> c p t d", t=TT, p=P)

    with Scope(nc, "wav") as s:
        ident = s.sb("ident", [P, P])
        w_nat = s.sb("w_nat", [P, 3, P])
        w_T = s.sb("w_T", [P, 3, P])
        wqv_rows = s.sb("wqv_rows", [M, 2, P])
        wqv_c = s.sb("wqv_c", [P, 2 * M])
        w_c = s.sb("w_c", [P, M])
        coef = s.sb("coef", [P, M])
        bias_q = s.sb("bias_q", [P, 1])
        bias_v = s.sb("bias_v", [P, 1])
        bias_o = s.sb("bias_o", [1, P])
        ones = s.sb("ones", [1, P])
        xin = [s.sb(f"xin{u}", [P, TT, P]) for u in range(2)]
        xT = [s.sb(f"xT{u}", [P, CH]) for u in range(2)]
        qv = [s.sb(f"qv{u}", [P, 2, CH]) for u in range(2)]
        a1 = s.sb("a1", [P, 2, CH // 2])
        d1 = s.sb("d1", [P, 2, CH // 2])
        a2 = s.sb("a2", [P, 2, CH // 4])
        d2 = s.sb("d2", [P, 2, CH // 4])
        a3 = s.sb("a3", [P, 2, CH // 8])
        d3 = s.sb("d3", [P, 2, CH // 8])
        p0 = s.sb("p0", [P, CH // 8])
        p1 = s.sb("p1", [P, CH // 8])
        p2 = s.sb("p2", [P, CH // 4])
        p3 = s.sb("p3", [P, CH // 2])
        r1 = s.sb("r1", [P, CH // 4])
        r2 = s.sb("r2", [P, CH // 2])
        mixed = [s.sb(f"mixed{u}", [P, CH]) for u in range(2)]
        stats = s.sb("stats", [P, TT, 6])
        mv = s.sb("mv", [P, TT, 2])
        std = s.sb("std", [P, TT])
        rstd = s.sb("rstd", [P, TT])
        eps = s.sb("eps", [P, 1])
        x1 = [s.sb(f"x1{u}", [P, TT, P]) for u in range(2)]
        ps_w = s.ps("ps_w", [P, 512])
        ps_x = s.ps("ps_x", [P, CH])
        ps_q = s.ps("ps_q", [P, CH])
        ps_v = s.ps("ps_v", [P, CH])
        ps_o = [s.ps(f"ps_o{u}", [P, CH]) for u in range(2)]

        w_loaded, x_loaded = s.sem("w_loaded"), [s.sem(f"x_loaded{u}") for u in range(2)]
        zeroed, ident_made, eps_set = s.sem("zeroed"), s.sem("ident_made"), s.sem("eps_set")
        wT_ready, wT_copied = s.sem("wT_ready"), s.sem("wT_copied")
        x_free = s.sem("x_free")
        xT_ready, xT_copied = s.sem("xT_ready"), s.sem("xT_copied")
        qv_ready, qv_copied = s.sem("qv_ready"), s.sem("qv_copied")
        mixed_ready, o_ready = s.sem("mixed_ready"), s.sem("o_ready")
        step = s.sem("step")
        var_ready, std_ready, x1_ready = s.sem("var_ready"), s.sem("std_ready"), s.sem("x1_ready")
        stats_ready = s.sem("stats_ready")
        rstd_ready, wqv_copied = s.sem("rstd_ready"), s.sem("wqv_copied")
        passed = s.sem("passed")
        x1_free = s.sem("x1_free")
        stored = [s.sem(f"stored{u}") for u in range(2)]
        block = s.stack.enter_context(nc.Block())
        loads = [(w_nat[:, 0, :], W_qkv[0:D, :]), (w_nat[:, 1, :], W_qkv[2 * D:3 * D, :]), (w_nat[:, 2, :], W_out),
                 (bias_q[:, :], column(b_qkv[0:D])), (bias_v[:, :], column(b_qkv[2 * D:3 * D])),
                 (bias_o[:, :], b_out.rearrange("(a m) -> a m", a=1))]
        for k, w in enumerate((weight_q, weight_v)):
            loads.append((wqv_rows[:, k, :].rearrange("m (h d) -> m h d", h=H), w.rearrange("h m d -> m h d")))
        n_w = 16 * len(loads)
        PAIRS = chunks // 2 - 1

        @block.sync
        def _(sp):
            with sp.Fori(0, chunks // 2) as i:
                for u in range(2):
                    c = i * 2 + u
                    sp.wait_ge(x_free, c + 1)
                    sp.dma_start(xin[u][:, :, :], x_t[bass.ds(c, 1)].rearrange("c p t d -> (c p) t d")).then_inc(x_loaded[u], 16)

        @block.gpsimd
        def _(pool):
            make_identity(pool, ident, zeroed, ident_made)
            pool.memset(eps[:, :], EPS).then_inc(eps_set, 1)
            pool.memset(ones[:, :], 1.0).then_inc(eps_set, 1)
            pool.sem_inc(x1_free, 2)
            with pool.Fori(0, chunks // 2) as i:
                for u in range(2):
                    c = i * 2 + u
                    pool.wait_ge(x1_ready, c + 1)
                    pool.dma_start(x1_t[bass.ds(c, 1)].rearrange("c p t d -> (c p) t d"), x1[u][:, :, :]).then_inc(stored[u], 16)
                    pool.wait_ge(stored[u], i * 16 + 16)
                    pool.sem_inc(x1_free, 1)

        @block.tensor
        def _(pe):
            def turn(c, u):
                pe.wait_ge(x_loaded[u], c * 8 + (16 - 8 * u))
                if not isinstance(c, int) or c:
                    pe.wait_ge(xT_copied, c)
                for t in range(TT):
                    last = pe.transpose(ps_x[:, t * P:(t + 1) * P], xin[u][:, t, :], ident[:, :])
                last.then_inc(xT_ready, 1)

            pe.wait_ge(ident_made, 1)
            turn(0, 0)
            pe.wait_ge(w_loaded, n_w)
            for k in range(3):
                pe.transpose(ps_w[:, k * P:(k + 1) * P], w_nat[:, k, :], ident[:, :])
            for k in range(2):
                last = pe.transpose(ps_w[:, 3 * P + k * M:3 * P + (k + 1) * M], wqv_rows[:, k, :], ident[0:M, 0:M])
            last.then_inc(wT_ready, 1)
            pe.wait_ge(wT_copied, 1)
            pe.wait_ge(eps_set, 2)
            def project(c, u):
                pe.wait_ge(xT_copied, c + 1)
                if not isinstance(c, int) or c:
                    pe.wait_ge(qv_copied, c * 2)
                pe.matmul(ps_q[:, :], w_T[:, 0, :], xT[u][:, :], start=True, stop=True).then_inc(qv_ready, 1)
                pe.matmul(ps_v[:, :], w_T[:, 1, :], xT[u][:, :], start=True, stop=True).then_inc(qv_ready, 1)

            def finish(c, u):
                pe.wait_ge(mixed_ready, c + 1)
                for t in range(TT):
                    tile = slice(t * P, (t + 1) * P)
                    pe.matmul(ps_o[u][:, tile], mixed[u][:, tile], w_T[:, 2, :], start=True, stop=False)
                    pe.matmul(ps_o[u][:, tile], ones[:, :], bias_o[:, :], start=False, stop=False)
                    last = pe.matmul(ps_o[u][:, tile], xT[u][:, tile], ident[:, :], start=False, stop=True)
                last.then_inc(o_ready, 1)

            project(0, 0)
            turn(1, 1)
            project(1, 1)
            with pe.Fori(0, PAIRS) as i:
                for u in range(2):
                    c = i * 2 + u
                    turn(c + 2, u)
                    finish(c, u)
                    project(c + 2, u)
            finish(chunks - 2, 0)
            finish(chunks - 1, 1)

        @block.scalar
        def _(act):
            def front(c, u):
                act.wait_ge(xT_ready, c + 1)
                if not isinstance(c, int):
                    act.wait_ge(o_ready, c - 1)
                act.activation(xT[u][:, :], ps_x[:, :], ACT.Copy).then_inc(xT_copied, 1)
                act.wait_ge(xT_copied, c + 1)
                act.sem_inc(x_free, 1)
                if isinstance(c, int) and c == 0:
                    act.wait_ge(w_loaded, n_w)
                act.wait_ge(qv_ready, c * 2 + 1)
                act.activation(qv[u][:, 0, :], ps_q[:, :], ACT.Identity, bias=bias_q[:, :]).then_inc(qv_copied, 1)
                act.wait_ge(qv_ready, c * 2 + 2)
                act.activation(qv[u][:, 1, :], ps_v[:, :], ACT.Identity, bias=bias_v[:, :]).then_inc(qv_copied, 1)

            def root(c):
                act.wait_ge(var_ready, c + 1)
                act.activation(std[:, :], mv[:, :, 1], ACT.Sqrt, bias=eps[:, :]).then_inc(std_ready, 1)

            act.sem_inc(x_free, 2)
            for dst, src in loads:
                act.dma_start(dst, src).then_inc(w_loaded, 16)
            act.wait_ge(eps_set, 2)
            front(0, 0)
            front(1, 1)
            with act.Fori(0, PAIRS) as i:
                for u in range(2):
                    front(i * 2 + (u + 2), u)
                    root(i * 2 + u)
            root(chunks - 2)
            root(chunks - 1)

        @block.vector
        def _(dve):
            dve.wait_ge(w_loaded, n_w)
            dve.wait_ge(wT_ready, 1)
            dve.tensor_copy(wqv_c[:, :], ps_w[:, 3 * P:3 * P + 2 * M]).then_inc(wqv_copied, 1)
            dve.tensor_copy(w_T[:, :, :].rearrange("p k n -> p (k n)"), ps_w[:, 0:3 * P]).then_inc(wT_copied, 1)
            dve.wait_ge(wqv_copied, 1)
            dve.tensor_tensor(w_c[:, :], wqv_c[:, 0:M], wqv_c[:, M:2 * M], ALU.mult).then_inc(step, 1)
            dve.wait_ge(step, 1)
            dve.tensor_scalar(coef[:, 0:2], w_c[:, 0:2], S ** 9, None, ALU.mult).then_inc(step, 1)
            dve.tensor_scalar(coef[:, 2:3], w_c[:, 2:3], S ** 6, None, ALU.mult).then_inc(step, 1)
            STEPS = 16

            def wavelet(c, u):
                at = c * STEPS + 3
                q = qv[u]
                dve.wait_ge(qv_copied, c * 2 + 2)
                dve.wait_ge(step, at)
                dve.tensor_tensor(a1[:, :, :], q[:, :, 0::2], q[:, :, 1::2], ALU.add).then_inc(step, 1)
                dve.tensor_tensor(d1[:, :, :], q[:, :, 0::2], q[:, :, 1::2], ALU.subtract).then_inc(step, 1)
                dve.wait_ge(step, at + 1)
                dve.tensor_tensor(a2[:, :, :], a1[:, :, 0::2], a1[:, :, 1::2], ALU.add).then_inc(step, 1)
                dve.tensor_tensor(d2[:, :, :], a1[:, :, 0::2], a1[:, :, 1::2], ALU.subtract).then_inc(step, 1)
                dve.wait_ge(step, at + 3)
                dve.tensor_tensor(a3[:, :, :], a2[:, :, 0::2], a2[:, :, 1::2], ALU.add).then_inc(step, 1)
                dve.tensor_tensor(d3[:, :, :], a2[:, :, 0::2], a2[:, :, 1::2], ALU.subtract).then_inc(step, 1)
                dve.scalar_tensor_tensor(out=p3[:, :], in0=d1[:, 0, :], scalar=S ** 3, in1=d1[:, 1, :],
                                         op0=ALU.mult, op1=ALU.mult).then_inc(step, 1)
                dve.wait_ge(step, at + 4)
                dve.scalar_tensor_tensor(out=p2[:, :], in0=d2[:, 0, :], scalar=coef[:, 2:3], in1=d2[:, 1, :],
                                         op0=ALU.mult, op1=ALU.mult).then_inc(step, 1)
                dve.wait_ge(step, at + 6)
                dve.scalar_tensor_tensor(out=p1[:, :], in0=d3[:, 0, :], scalar=coef[:, 1:2], in1=d3[:, 1, :],
                                         op0=ALU.mult, op1=ALU.mult).then_inc(step, 1)
                dve.scalar_tensor_tensor(out=p0[:, :], in0=a3[:, 0, :], scalar=coef[:, 0:1], in1=a3[:, 1, :],
                                         op0=ALU.mult, op1=ALU.mult).then_inc(step, 1)
                dve.wait_ge(step, at + 10)
                dve.tensor_tensor(r1[:, 0::2], p0[:, :], p1[:, :], ALU.add).then_inc(step, 1)
                dve.tensor_tensor(r1[:, 1::2], p0[:, :], p1[:, :], ALU.subtract).then_inc(step, 1)
                dve.wait_ge(step, at + 12)
                dve.tensor_tensor(r2[:, 0::2], r1[:, :], p2[:, :], ALU.add).then_inc(step, 1)
                dve.tensor_tensor(r2[:, 1::2], r1[:, :], p2[:, :], ALU.subtract).then_inc(step, 1)
                dve.wait_ge(step, at + 14)
                dve.tensor_tensor(mixed[u][:, 0::2], r2[:, :], p3[:, :], ALU.add).then_inc(step, 1)
                dve.tensor_tensor(mixed[u][:, 1::2], r2[:, :], p3[:, :], ALU.subtract).then_inc(step, 1)
                dve.wait_ge(step, at + 16)
                dve.sem_inc(mixed_ready, 1)

            def normalize(c, u):
                dve.wait_ge(o_ready, c + 1)
                for t in range(TT):
                    last = dve.bn_stats(stats[:, t, :], ps_o[u][:, t * P:(t + 1) * P])
                last.then_inc(stats_ready, 1)
                dve.wait_ge(stats_ready, c + 1)
                pass_wait(dve, passed)
                for t in range(TT):
                    last = dve.bn_aggr(mv[:, t, :], stats[:, t, :])
                last.then_inc(var_ready, 1)
                dve.wait_ge(std_ready, c + 1)
                dve.reciprocal(rstd[:, :], std[:, :]).then_inc(rstd_ready, 1)
                dve.wait_ge(rstd_ready, c + 1)
                dve.wait_ge(x1_free, c + 1)
                for t in range(TT):
                    last = dve.tensor_scalar(x1[u][:, t, :], ps_o[u][:, t * P:(t + 1) * P], mv[:, t, 0:1], rstd[:, t:t + 1],
                                             ALU.subtract, ALU.mult)
                last.then_inc(x1_ready, 1)

            wavelet(0, 0)
            with dve.Fori(0, PAIRS) as i:
                for u in range(2):
                    wavelet(i * 2 + (u + 1), 1 - u)
                    normalize(i * 2 + u, u)
            wavelet(chunks - 1, 1)
            normalize(chunks - 2, 0)
            normalize(chunks - 1, 1)


class CrossShapes:
    G, HG, DH, LAG, RING = 4, 4, 8, 3, 4
    MASKED = 72
    TOP = 96
    DVE_TILES = (6, 8, 10, 12)
    FILLS = ((0, 9), (0, 10), (0, 12), (1, 1))
    SWEEPS = ((0, 1), (2, 3), (4, 5), (6, 7), (8, 9), (10, 11), (12,), (13, 14), (15,), (), (), (), ())


def cross_jobs(first, last):
    jobs = {(g, t): [] for g in range(4) for t in range(13)}
    jobs[0, 2].append("f5")
    jobs[0, 3].append("f6")
    if not first:
        jobs[0, 5].append("den3")
        jobs[0, 7].append("out")
    for g in range(3):
        jobs[g + 1, 10 if g else 5].append(f"den{g}")
    if not last:
        for k, slot in enumerate([(0, 4), (0, 6), (0, 8), (0, 10)]):
            jobs[slot].append(f"ctx{k}")
        for k, slot in enumerate([(0, 11), (0, 12), (1, 0), (1, 1)]):
            jobs[slot].append(f"k{k}")
        for k, slot in enumerate([(1, 12), (2, 4), (2, 12), (3, 3)]):
            jobs[slot].append(f"v{k}")
        jobs[1, 2].append("x1")
        jobs[1, 3].append("q")
        jobs[1, 4].append("count")
        jobs[1, 8].append("total")
        jobs[1, 10].append("row")
        for k in range(5):
            jobs[3, (5, 7, 8, 11, 12)[k]].append(f"f{k}")
    for g in range(4):
        if not (last and g == 3):
            jobs[g, 9].insert(0, "top")
    return jobs


PREPARE = (["ctx0", "ctx1", "ctx2", "ctx3", "x1"] + [f"k{k}" for k in range(4)]
           + ["q", "count", "total", "row"] + [f"v{k}" for k in range(4)] + [f"f{k}" for k in range(5)] + ["top"])


def cross_pass(nc, ctx, gate, mask, wq, bq, wk, bk, wv, bv, wo, bo, x1_dram, y2_dram):
    C = CrossShapes
    B, SK, D = ctx.shape
    SQ = gate.shape[1]
    QT = SQ // P
    KT = -(-SK // P)
    PK = KT * P
    REST = SK - (KT - 1) * P
    HALF = (SK - SK // 2, SK // 2)
    G, HG, DH, LAG, RING, MASKED, TOP = C.G, C.HG, C.DH, C.LAG, C.RING, C.MASKED, C.TOP
    H = G * HG
    UNITS = HG * QT * 2
    NEG = -998244352.0
    TWO_ONES = 1.0019378662109375
    SCALE = DH ** -0.5
    VW = H * (DH + 1) + 24
    SLOTS = G * KT
    N_DVE = len(C.DVE_TILES)
    N_POOL = KT - N_DVE

    with Scope(nc, "x") as s:
        ident = s.sb("ident", [P, P])
        ident_bf = s.sb("ident_bf", [P, P], BF16)
        ones = s.sb("ones", [P, P])
        ones_bf = s.sb("ones_bf", [P, 1], BF16)
        spread = s.sb("spread", [P, P])
        w_nat = s.sb("w_nat", [P, 2, P])
        w_sb = s.sb("w_sb", [P, 2, P])
        wv_sb = s.sb("wv_sb", [P, P])
        wo_sb = s.sb("wo_sb", [P, G, P])
        b_rows = s.sb("b_rows", [1, 2, P])
        b_perm = s.sb("b_perm", [1, 2, P])
        b_qk = s.sb("b_qk", [P, 2])
        bv_sb = s.sb("bv_sb", [P, P])
        bo_sb = s.sb("bo_sb", [P, P])
        nat = s.sb("nat", [P, QT, SK])
        nat_int = nat[:, :, :].bitcast(I32)
        ctx_nat = s.sb("ctx_nat", [P, KT, P])
        k_f = ctx_nat[:, :, :].rearrange("p t d -> p (t d)")
        ctx_T = s.sb("ctx_T", [P, PK])
        k_part = [s.sb(f"k_part{n}", [P, PK], BF16) for n in range(3)]
        q_f = s.sb("q_f", [P, SQ])
        q_part = [s.sb(f"q_part{n}", [P, SQ], BF16) for n in range(3)]
        k_aug = s.sb("k_aug", [P, H, PK], BF16)
        q_aug = [s.sb(f"q_aug{u}", [P, H, SQ], BF16) for u in range(2)]
        neg = [s.sb(f"neg{u}", [P, QT, PK], BF16) for u in range(2)]
        gate_T = s.sb("gate_T", [P, KT, SQ])
        values = [s.sb(f"values{u}", [P, KT, VW]) for u in range(2)]
        x1_nat = [s.sb(f"x1_nat{u}", [P, QT, D]) for u in range(2)]
        x1_T = s.sb("x1_T", [P, SQ])
        weights = [s.sb(f"weights{r}", [P, HG, 2 * SQ]) for r in range(RING)]
        swept = [s.sb(f"swept{u}", [P, HALF[0]], BF16) for u in range(2)]
        top2 = s.sb("top2", [P, HG * QT, 2])
        top = s.sb("top", [P, HG * QT])
        top_r = s.sb("top_r", [HG * QT, P])
        top_part = [s.sb(f"top_part{n}", [HG * QT, P], BF16) for n in range(3)]
        seen = s.sb("seen", [P, 2, KT])
        seen_n = s.sb("seen_n", [P, 2])
        whole = s.sb("whole", [P, 2])
        fast = s.sb("fast", [P, 1])
        row_c = s.sb("row_c", [P, 2 * HG, KT])
        row_bf = s.sb("row_bf", [HG * KT, P], BF16)
        general = [s.sb(f"general{u}", [P, 1], I32) for u in range(2)]
        o_sb = s.sb("o_sb", [P, 2 * SQ])
        total_sb = s.sb("total_sb", [P, SQ])
        inv = s.sb("inv", [P, SQ])
        o_T = s.sb("o_T", [P, G, SQ])
        y2 = s.sb("y2", [P, QT, D])

        ps_s = [s.ps(f"ps_s{u}", [P, 2 * SQ]) for u in range(2)]
        ps_m = [s.ps(f"ps_m{u}", [P, 1024]) for u in range(2)]
        ps_o = s.ps("ps_o", [P, 2 * SQ])
        ps_misc = s.ps("ps_misc", [P, 512])

        w_loaded, zeroed, made, set_dve = s.sem("w_loaded"), s.sem("zeroed"), s.sem("made"), s.sem("set_dve")
        b_turned, b_ready = s.sem("b_turned"), s.sem("b_ready")
        x1_loaded = [s.sem(f"x1_loaded{u}") for u in range(2)]
        ctx_loaded, mask_loaded, gate_loaded = s.sem("ctx_loaded"), s.sem("mask_loaded"), s.sem("gate_loaded")
        q_loaded = [s.sem(f"q_loaded{u}") for u in range(2)]
        k_loaded = [s.sem(f"k_loaded{g}") for g in range(G)]
        top_loaded = [s.sem(f"top_loaded{g}") for g in range(2)]
        y2_stored = s.sem("y2_stored")
        misc_ready, misc_read = s.sem("misc_ready"), s.sem("misc_read")
        s_ready = s.sem("s_ready")
        exp_ready = s.sem("exp_ready")
        gated_dve, gated_pool = s.sem("gated_dve"), s.sem("gated_pool")
        applied = s.sem("applied")
        o_copied = s.sem("o_copied")
        o_normed = s.sem("o_normed")
        m_ready = s.sem("m_ready")
        m_read = s.sem("m_read")
        inv_ready = s.sem("inv_ready")
        top_ready, top_step, top_split = s.sem("top_ready"), s.sem("top_step"), s.sem("top_split")
        part_made = [s.sem(f"part_made{n}") for n in range(3)]
        rest_made = [s.sem(f"rest_made{n}") for n in range(2)]
        neg_made, general_made = s.sem("neg_made"), s.sem("general_made")
        seen_ready, fast_ready, row_ready = s.sem("seen_ready"), s.sem("fast_ready"), s.sem("row_ready")
        y2_ready = s.sem("y2_ready")
        passed = s.sem("passed")
        N_SET = 10

        block = s.stack.enter_context(nc.Block())
        x1_t = x1_dram.rearrange("(b t p) d -> b p t d", t=QT, p=P)
        y2_t = y2_dram.rearrange("(b t p) d -> b p t d", t=QT, p=P)
        gate_t = gate.rearrange("b (t p) k -> b p t k", t=QT)
        mask_t = mask.rearrange("b (t p) k -> b p t k", t=QT)

        def one(ap, b):
            return ap[b] if isinstance(b, int) else ap[bass.ds(b, 1)].rearrange("b p t k -> (b p) t k")

        first_jobs, inner_jobs, last_jobs = cross_jobs(True, False), cross_jobs(False, False), cross_jobs(False, True)
        n_first = sum(len(v) for v in first_jobs.values())
        n_inner = sum(len(v) for v in inner_jobs.values())

        def job_numbers(jobs, b, is_first):
            base = len(PREPARE) if is_first else (b - 1) * n_inner + (len(PREPARE) + n_first)
            number, k = {}, 0
            for slot, names in jobs.items():
                for place in range(len(names)):
                    number[slot, place] = base + k
                    k += 1
            return number, base + k

        def cycles(eng, prologue, cycle, epilogue):
            prologue()
            cycle(0, 0, first_jobs, True, False)
            with eng.Fori(0, (B - 2) // 2) as i:
                for v in range(2):
                    cycle(i * 2 + (1 + v), (1 + v) % 2, inner_jobs, False, False)
            cycle(B - 1, (B - 1) % 2, last_jobs, False, True)
            epilogue()

        def walk(jobs, b, is_first):
            number, _ = job_numbers(jobs, b, is_first)
            for g in range(G):
                for t in range(KT):
                    yield g, t, b * SLOTS + (g * KT + t), [(number[(g, t), k], j) for k, j in enumerate(jobs[g, t])]

        END_JOB = len(PREPARE) + n_first + (B - 2) * n_inner + sum(len(v) for v in last_jobs.values())

        @block.sync
        def _(sp):
            wl = [(w_nat[:, 0, :], wq), (w_nat[:, 1, :], wk), (wv_sb[:, :], wv), (bv_sb[:, :], row_bcast(bv)),
                  (bo_sb[:, :], row_bcast(bo)), (b_rows[:, 0, :], bq.rearrange("(a m) -> a m", a=1)),
                  (b_rows[:, 1, :], bk.rearrange("(a m) -> a m", a=1))]
            for dst, src in wl:
                sp.dma_start(dst, src).then_inc(w_loaded, 16)
            sp.wait_ge(made, 6)
            for j in range(HG):
                sp.dma_start(wo_sb[32 * j:32 * j + DH, :, :],
                             wo.rearrange("(g j d) n -> j d g n", g=G, j=HG)[j]).then_inc(w_loaded, 16)

            def place_k_part(g, n):
                for c in (3 * n, 3 * n + 1, 3 * n + 2):
                    sp.dma_start(k_aug[DH * c:DH * c + DH, HG * g:HG * g + HG, :], k_part[n][32 * g:32 * g + 32, :])\
                      .then_inc(k_loaded[g], 16)

            def place_row(g):
                sp.dma_start(k_aug[MASKED:MASKED + 1, HG * g:HG * g + HG, :], row_bf[:, :]).then_inc(k_loaded[g], 16)

            def place_q_part(u, n):
                for c in (n, n + 3, n + 6):
                    sp.dma_start(q_aug[u][DH * c:DH * c + DH, :, :], q_part[n][:, :]).then_inc(q_loaded[u], 16)

            def place_k(b, g):
                if not (isinstance(b, int) and b == 0):
                    sp.wait_ge(s_ready, (b - 1) * (2 * SLOTS) + 2 * KT * (g + 1))
                    pass_wait(sp, passed)
                sp.wait_ge(part_made[2], b + 1)
                for n in range(3):
                    place_k_part(g, n)
                place_row(g)

            def place_q(b, u):
                sp.wait_ge(part_made[2], b + 1)
                for n in range(3):
                    place_q_part(u, n)

            def place_top(b, g, u):
                sp.wait_ge(top_split, b * G + (g + 1))
                for n in range(3):
                    sp.dma_start(q_aug[u][TOP + n:TOP + n + 1, HG * g:HG * g + HG, :], top_part[n][:, :])\
                      .then_inc(top_loaded[g % 2], 16)

            def prologue():
                sp.wait_ge(made, 8)
                sp.wait_ge(set_dve, N_SET)
                for n in range(3):
                    sp.wait_ge(part_made[n], 1)
                    place_q_part(0, n)
                    place_k_part(0, n)
                place_row(0)
                place_k(0, 1)
                place_k(0, 2)
                place_top(0, 0, 0)

            def cycle(b, u, jobs, is_first, is_last):
                place_k(b, 3)
                place_top(b, 1, u)
                place_top(b, 2, u)
                if not is_last:
                    place_q(b + 1, 1 - u)
                    place_k(b + 1, 0)
                    place_k(b + 1, 1)
                place_top(b, 3, u)
                if not is_last:
                    place_k(b + 1, 2)
                    place_top(b + 1, 0, 1 - u)

            cycles(sp, prologue, cycle, lambda: None)

        @block.gpsimd
        def _(pool):
            pool.memset(ident[:, :], 0.0).then_inc(zeroed, 1)
            pool.memset(spread[:, :], 0.0).then_inc(zeroed, 1)
            pool.wait_ge(zeroed, 2)
            pool.affine_select(out=ident[:, :], in_=ident[:, :], compare_op=ALU.not_equal, fill=1.0,
                               base=0, pattern=[[-1, P]], channel_multiplier=1).then_inc(made, 1)
            by_head = spread[:, :].rearrange("p (j m) -> p j m", j=HG)
            pool.affine_select(out=by_head, in_=by_head, compare_op=ALU.not_equal, fill=1.0,
                               base=-DH, pattern=[[-32, HG], [0, 32]], channel_multiplier=1).then_inc(made, 1)
            pool.memset(ones[:, :], 1.0).then_inc(made, 1)
            pool.memset(ones_bf[:, :], 1.0).then_inc(made, 1)
            pool.wait_ge(made, 1)
            pool.tensor_copy(ident_bf[:, :], ident[:, :]).then_inc(made, 1)
            pool.memset(wo_sb[:, :, :], 0.0).then_inc(made, 1)
            pool.wait_ge(made, 6)
            pool.memset(k_aug[64:TOP, :, :].bitcast(F32), 0.0).then_inc(made, 1)
            pool.wait_ge(made, 7)
            pool.memset(k_aug[TOP:P, :, :].bitcast(F32), TWO_ONES).then_inc(made, 1)

            def remainder(b, n):
                pool.wait_ge(part_made[n], b + 1)
                pool.tensor_tensor(q_f[:, :], q_f[:, :], q_part[n][:, :], ALU.subtract)
                pool.tensor_tensor(k_f, k_f, k_part[n][:, :], ALU.subtract).then_inc(rest_made[n], 1)

            def prologue():
                pool.wait_ge(made, 8)
                remainder(0, 0)
                remainder(0, 1)

            def cycle(b, u, jobs, is_first, is_last):
                for g, t, n, _ in walk(jobs, b, is_first):
                    if t not in C.DVE_TILES:
                        pool.wait_ge(exp_ready, n * 2 + 4)
                        w = weights[(g * KT + t) % RING]
                        pool.tensor_tensor(w[:, :, 0:SQ], w[:, :, SQ:],
                                           gate_T[:, t, :].unsqueeze(1).to_broadcast([P, HG, SQ]), ALU.mult)\
                            .then_inc(gated_pool, 1)
                    if not is_last and (g, t) == (1, 4):
                        remainder(b + 1, 0)
                    if not is_last and (g, t) == (1, 7):
                        remainder(b + 1, 1)

            cycles(pool, prologue, cycle, lambda: None)

        @block.scalar
        def _(act):
            def load_mask(b):
                act.dma_start(nat_int, one(mask_t, b)).then_inc(mask_loaded, 16)

            def load_gate(b):
                act.dma_start(nat[:, :, :], one(gate_t, b)).then_inc(gate_loaded, 16)

            def load_ctx(b):
                c = ctx[b] if isinstance(b, int) else ctx[bass.ds(b, 1)].rearrange("b k d -> (b k) d")
                act.dma_start(ctx_nat[:, 0:KT - 1, :], c[0:(KT - 1) * P, :].rearrange("(t p) d -> p t d", p=P))\
                   .then_inc(ctx_loaded, 16)
                act.dma_start(ctx_nat[0:REST, KT - 1, :], c[(KT - 1) * P:SK, :]).then_inc(ctx_loaded, 16)

            def load_x1(b, u):
                act.dma_start(x1_nat[u][:, :, :], one(x1_t, b)).then_inc(x1_loaded[u], 16)

            def mine(name):
                return name[0] in "fk" or name in ("x1", "q", "row") or name[:3] in ("ctx", "den")

            def copy_job(J, name):
                k = int(name[-1]) if name[-1].isdigit() else 0
                act.wait_ge(misc_ready, J + 1)
                if name[0] == "f" and k < 6:
                    act.activation(gate_T[:, 2 * k:2 * k + 2, :].rearrange("p t q -> p (t q)"), ps_misc[:, :],
                                   ACT.Copy).then_inc(misc_read, 1)
                elif name == "f6":
                    act.activation(gate_T[0:REST, KT - 1, :], ps_misc[0:REST, 0:SQ], ACT.Copy).then_inc(misc_read, 1)
                elif name[:3] == "ctx":
                    n = 4 * P if k < 3 else REST
                    act.activation(ctx_T[:, 4 * P * k:4 * P * k + n], ps_misc[:, 0:n], ACT.Copy).then_inc(misc_read, 1)
                elif name[:3] == "den":
                    act.activation(total_sb[:, :], ps_misc[:, 0:SQ], ACT.Copy).then_inc(misc_read, 1)
                elif name == "x1":
                    act.activation(x1_T[:, :], ps_misc[:, 0:SQ], ACT.Copy).then_inc(misc_read, 1)
                elif name[0] == "k":
                    n = PK // 4
                    act.activation(k_f[:, n * k:n * k + n], ps_misc[:, 0:n], ACT.Identity, bias=b_qk[:, 1:2])\
                       .then_inc(misc_read, 1)
                elif name == "q":
                    act.activation(q_f[:, :], ps_misc[:, 0:SQ], ACT.Identity, bias=b_qk[:, 0:1], scale=SCALE)\
                       .then_inc(misc_read, 1)
                elif name == "row":
                    act.activation(row_bf[:, :], ps_misc[0:HG * KT, 0:P], ACT.Copy).then_inc(misc_read, 1)

            def part(b, n, half, copied=0, u=0):
                lo, hi = half * PK // 2, (half + 1) * PK // 2
                if half:
                    act.activation(k_part[n][:, lo:hi], k_f[:, lo:hi], ACT.Copy).then_inc(part_made[n], 1)
                    return
                if n:
                    act.wait_ge(rest_made[n - 1], b + 1)
                else:
                    act.wait_ge(misc_read, copied)
                    if not (isinstance(b, int) and b == 0):
                        for g in range(G):
                            act.wait_ge(k_loaded[g], b * (10 * 16))
                        act.wait_ge(q_loaded[1 - u], b * (9 * 8) + u * (9 * 8))
                act.activation(q_part[n][:, :], q_f[:, :], ACT.Copy)
                act.activation(k_part[n][:, lo:hi], k_f[:, lo:hi], ACT.Copy)

            def fill(b, u, piece):
                t, lo, hi = piece // 2, piece % 2 * HALF[0], SK if piece % 2 else HALF[0]
                act.wait_ge(mask_loaded, b * 16 + 16)
                act.activation(neg[u][:, t, lo:hi], nat_int[:, t, lo:hi], ACT.Copy, scale=-NEG, bias=NEG).then_inc(neg_made, 1)

            def next_gate(b):
                act.wait_ge(neg_made, b * (2 * QT) + 2 * QT)
                load_gate(b)

            def copy_sums(c, n):
                act.wait_ge(applied, n + (1 - LAG + RING))
                act.wait_ge(o_normed, c)
                act.activation(o_sb[:, :], ps_o[:, :], ACT.Copy).then_inc(o_copied, 1)

            def store(b):
                act.wait_ge(y2_ready, b + 1)
                act.dma_start(one(y2_t, b), y2[:, :, :]).then_inc(y2_stored, 16)

            def prologue():
                act.sem_inc(exp_ready, 2)
                act.sem_inc(o_copied, 1)
                load_ctx(0)
                load_x1(0, 0)
                load_mask(0)
                for J, name in enumerate(PREPARE):
                    if name == "k0":
                        act.wait_ge(b_ready, 2)
                    if mine(name):
                        copy_job(J, name)
                    if name == "q":
                        part(0, 0, 0, J + 1)
                        part(0, 0, 1)
                        for piece in range(2 * QT):
                            fill(0, 0, piece)
                        next_gate(0)
                        for half in range(2):
                            part(0, 1, half)
                    if name == "row":
                        for half in range(2):
                            part(0, 2, half)

            def cycle(b, u, jobs, is_first, is_last):
                for g, t, n, todo in walk(jobs, b, is_first):
                    if (g, t) == (0, 0) and not is_last:
                        act.wait_ge(part_made[2], b + 1)
                        load_ctx(b + 1)
                    if t == LAG and not (is_first and g == 0):
                        copy_sums(b * G + (g - 1), n - 1)
                    w = weights[(g * KT + t) % RING]
                    act.wait_ge(applied, n + 1)
                    for pair in range(2):
                        act.wait_ge(s_ready, n * 2 + (pair + 1))
                        act.activation(w[:, 2 * pair:2 * pair + 2, SQ:], ps_s[pair][:, :].rearrange("p (h q) -> p h q", h=2),
                                       ACT.Exp).then_inc(exp_ready, 1)
                    for J, name in todo:
                        if name in ("f0", "f1", "f2", "f3", "f4"):
                            upto = 2 * int(name[1]) + 1
                            mine_dve = sum(x <= upto for x in C.DVE_TILES)
                            act.wait_ge(gated_dve, b * (G * N_DVE) + (3 * N_DVE + mine_dve))
                            act.wait_ge(gated_pool, b * (G * N_POOL) + (3 * N_POOL + upto + 1 - mine_dve))
                        if name in ("f5", "f6"):
                            act.wait_ge(gated_dve, b * (G * N_DVE))
                            act.wait_ge(gated_pool, b * (G * N_POOL))
                        if mine(name):
                            copy_job(J, name)
                        if name == "q":
                            part(b + 1, 0, 0, J + 1, 1 - u)
                    if (g, t) == (0, 4) and not is_last:
                        load_mask(b + 1)
                    if (g, t) == (0, 10):
                        if not is_first:
                            store(b - 1)
                        if not is_last:
                            load_x1(b + 1, 1 - u)
                    if is_last:
                        continue
                    if (g, t) in C.FILLS:
                        fill(b + 1, 1 - u, C.FILLS.index((g, t)))
                    if (g, t) == (1, 2):
                        next_gate(b + 1)
                    if (g, t) == (1, 4):
                        part(b + 1, 0, 1)
                    if (g, t) in ((1, 6), (1, 7)):
                        part(b + 1, 1, t - 6)
                    if (g, t) in ((1, 10), (1, 11)):
                        part(b + 1, 2, t - 10)

            def epilogue():
                copy_sums(B * G - 1, B * SLOTS - 1 + LAG)
                copy_job(END_JOB, "den3")
                store(B - 1)
                act.wait_ge(y2_stored, 16 * B)

            cycles(act, prologue, cycle, epilogue)

        @block.vector
        def _(dve):
            def unit(b, g, u, k):
                h, qt, half = k // (2 * QT), k // 2 % QT, k % 2
                m = b * (G * UNITS) + (g * UNITS + k)
                lo, n = half * HALF[0], HALF[half]
                if k == 0:
                    dve.wait_ge(neg_made, b * (2 * QT) + 2 * QT)
                dve.wait_ge(m_ready, m + 1)
                pass_wait(dve, passed)
                dve.tensor_tensor_reduce(out=swept[k % 2][:, 0:n], in0=ps_m[k % 2][:, 0:n], in1=neg[u][:, qt, lo:lo + n],
                                         scale=1.0, scalar=-3.0e38, op0=ALU.add, op1=ALU.max,
                                         accum_out=top2[:, h * QT + qt, half:half + 1]).then_inc(m_read, 1)

            def join(b, g):
                dve.wait_ge(m_read, b * (G * UNITS) + ((g + 1) * UNITS + 2))
                dve.tensor_tensor(top[:, :], top2[:, :, 0], top2[:, :, 1], ALU.max).then_inc(top_ready, 1)

            def split(J, b, g):
                x = ps_misc[0:HG * QT, 0:P]
                c = b * G + g
                dve.wait_ge(misc_ready, J + 1)
                dve.tensor_scalar(top_part[0][:, :], x, -1.0, None, ALU.mult).then_inc(top_step, 1)
                dve.wait_ge(top_step, c * 2 + 1)
                dve.scalar_tensor_tensor(out=top_r[:, :], in0=x, scalar=-1.0, in1=top_part[0][:, :],
                                         op0=ALU.mult, op1=ALU.subtract).then_inc(misc_read, 1)
                dve.wait_ge(misc_read, J + 1)
                dve.tensor_copy(top_part[1][:, :], top_r[:, :]).then_inc(top_step, 1)
                dve.wait_ge(top_step, c * 2 + 2)
                dve.tensor_tensor(top_part[2][:, :], top_r[:, :], top_part[1][:, :], ALU.subtract).then_inc(top_split, 1)

            def count(J, b):
                dve.wait_ge(misc_ready, J + 1)
                dve.tensor_scalar(seen[:, 0, :], ps_misc[:, 0:KT], 0.0, None, ALU.is_equal)
                dve.tensor_scalar(seen[:, 1, :], ps_misc[:, 0:KT], SQ * NEG, None, ALU.is_le).then_inc(misc_read, 1)
                dve.wait_ge(misc_read, J + 1)
                dve.tensor_reduce(seen_n[:, :], seen[:, :, :], AX_X, ALU.add).then_inc(seen_ready, 1)

            def total(J, b, u):
                dve.wait_ge(misc_ready, J + 1)
                dve.tensor_reduce(whole[:, 0:1], ps_misc[:, 0:2], AX_X, ALU.add)
                dve.tensor_scalar(whole[:, 1:2], ps_misc[:, 0:1], 1.0, None, ALU.is_ge).then_inc(misc_read, 1)
                dve.wait_ge(misc_read, J + 1)
                dve.scalar_tensor_tensor(out=fast[:, :], in0=whole[:, 0:1], scalar=float(PK), in1=whole[:, 1:2],
                                         op0=ALU.is_ge, op1=ALU.mult).then_inc(fast_ready, 1)
                dve.wait_ge(fast_ready, b + 1)
                dve.tensor_scalar(row_c[:, :, :], seen[:, 1, :].unsqueeze(1).to_broadcast([P, 2 * HG, KT]), fast[:, 0:1], NEG, ALU.mult, ALU.mult).then_inc(row_ready, 1)
                dve.tensor_scalar(general[u][:, :], fast[:, :], -1.0, 1.0, ALU.mult, ALU.add).then_inc(general_made, 1)

            def add_bias(J, k, u):
                n = 4 if k < KT // 4 else KT % 4
                dve.wait_ge(misc_ready, J + 1)
                dve.tensor_tensor(values[u][:, 4 * k:4 * k + n, 0:H * (DH + 1)].rearrange("p t (h e) -> p t h e", h=H)[:, :, :, 0:DH],
                                  ps_misc[:, 0:n * P].rearrange("p (t h d) -> p t h d", t=n, h=H),
                                  bv_sb[:, :].rearrange("p (h d) -> p h d", h=H).unsqueeze(1).to_broadcast([P, n, H, DH]),
                                  ALU.add).then_inc(misc_read, 1)

            def normalize(J, c, g):
                dve.wait_ge(misc_read, J + 1)
                dve.reciprocal(inv[:, :], total_sb[:, :]).then_inc(inv_ready, 1)
                dve.wait_ge(inv_ready, c + 1)
                dve.tensor_tensor(o_T[:, g, :], o_sb[:, 0:SQ], inv[:, :], ALU.mult).then_inc(o_normed, 1)

            def residual(J, b, u):
                dve.wait_ge(misc_ready, J + 1)
                dve.wait_ge(y2_stored, b * 16)
                dve.tensor_tensor(y2[:, :, :], ps_misc[:, 0:QT * D].rearrange("p (t d) -> p t d", t=QT),
                                  bo_sb[:, :].unsqueeze(1).to_broadcast([P, QT, D]), ALU.add).then_inc(misc_read, 1)
                dve.wait_ge(misc_read, J + 1)
                dve.tensor_tensor(y2[:, :, :], y2[:, :, :], x1_nat[u][:, :, :], ALU.add).then_inc(y2_ready, 1)

            def prologue():
                dve.wait_ge(w_loaded, 16 * (7 + HG))
                for dst, src in ((b_perm, b_rows), (w_sb, w_nat)):
                    dve.tensor_copy(dst[:, 0, :].rearrange("p (d h) -> p h d", d=DH),
                                    src[:, 0, :].rearrange("p (h d) -> p h d", d=DH)).then_inc(set_dve, 1)
                    dve.tensor_copy(dst[:, 1, :].rearrange("p (g d a) -> p g a d", g=G, d=DH),
                                    src[:, 1, :].rearrange("p (g a d) -> p g a d", g=G, a=HG)).then_inc(set_dve, 1)
                dve.memset(ctx_T[:, SK:PK], 0.0).then_inc(set_dve, 1)
                dve.memset(gate_T[:, KT - 1, :], 0.0).then_inc(set_dve, 1)
                dve.wait_ge(b_turned, 1)
                dve.tensor_scalar(b_qk[:, 0:1], ps_o[:, 0:1], SCALE, None, ALU.mult).then_inc(b_ready, 1)
                dve.tensor_copy(b_qk[:, 1:2], ps_o[:, 1:2]).then_inc(b_ready, 1)
                for u in range(2):
                    dve.memset(q_aug[u][64:TOP, :, :].bitcast(F32), TWO_ONES).then_inc(set_dve, 1)
                for u in range(2):
                    dve.memset(neg[u][:, :, SK:PK], 4 * NEG)
                    dve.memset(values[u][:, :, :], 1.0).then_inc(set_dve, 1)
                dve.sem_inc(m_read, 2)
                dve.wait_ge(set_dve, N_SET)
                for J, name in enumerate(PREPARE):
                    if name[0] == "v":
                        add_bias(J, int(name[1]), 0)
                    if name == "count":
                        count(J, 0)
                    if name == "total":
                        total(J, 0, 0)
                    if name == "top":
                        for k in range(UNITS):
                            unit(0, 0, 0, k)
                        join(0, 0)
                        split(J, 0, 0)

            def cycle(b, u, jobs, is_first, is_last):
                for g, t, n, todo in walk(jobs, b, is_first):
                    ahead = (b, g + 1, u) if g < G - 1 else (b + 1, 0, 1 - u)
                    if not (is_last and g == G - 1):
                        for k in C.SWEEPS[t]:
                            unit(*ahead, k)
                    if t == 8 and not (is_last and g == G - 1):
                        join(*ahead[:2])
                    if t in C.DVE_TILES:
                        dve.wait_ge(exp_ready, n * 2 + 4)
                        w = weights[(g * KT + t) % RING]
                        dve.tensor_tensor(w[:, :, 0:SQ], w[:, :, SQ:],
                                          gate_T[:, t, :].unsqueeze(1).to_broadcast([P, HG, SQ]), ALU.mult)\
                           .then_inc(gated_dve, 1)
                    for J, name in todo:
                        if name[0] == "v":
                            add_bias(J, int(name[1]), 1 - u)
                        if name == "count":
                            count(J, b + 1)
                        if name == "total":
                            total(J, b + 1, 1 - u)
                        if name == "top":
                            split(J, *ahead[:2])
                        if name[:3] == "den":
                            normalize(J, b * G + (g - 1), int(name[3]))
                        if name == "out":
                            residual(J, b - 1, 1 - u)

            def epilogue():
                normalize(END_JOB, B * G - 1, G - 1)
                residual(END_JOB + 1, B - 1, (B - 1) % 2)

            cycles(dve, prologue, cycle, epilogue)

        @block.tensor
        def _(pe):
            def unit(b, g, u, k):
                h, qt, half = HG * g + k // (2 * QT), k // 2 % QT, k % 2
                m = b * (G * UNITS) + (g * UNITS + k)
                lo, n = half * HALF[0], HALF[half]
                if k == 0:
                    pe.wait_ge(k_loaded[g], b * (10 * 16) + 10 * 16)
                    pe.wait_ge(q_loaded[u], b * (9 * 8) + (2 - u) * (9 * 8))
                pe.wait_ge(m_read, m + 1)
                for x in (0, 512):
                    last = pe.matmul(ps_m[k % 2][:, x:min(x + 512, n)], q_aug[u][0:TOP, h, qt * P:(qt + 1) * P],
                                     k_aug[0:TOP, h, lo + x:lo + min(x + 512, n)], start=True, stop=True)
                last.then_inc(m_ready, 1)

            def scores(b, g, t, n, u, general_way):
                tile = slice(t * P, (t + 1) * P)
                if t == 0:
                    pe.wait_ge(top_loaded[g % 2], b * 96 + 48 * (g // 2 + 1))
                for pair in range(2):
                    pe.wait_ge(exp_ready, n * 2 + (pair + 1))
                    for j in range(2):
                        h = HG * g + 2 * pair + j
                        dst = ps_s[pair][:, j * SQ:(j + 1) * SQ]
                        if not general_way:
                            last = pe.matmul(dst, k_aug[0:TOP + 3, h, tile], q_aug[u][0:TOP + 3, h, :], start=True, stop=True)
                            continue
                        pe.matmul(dst, k_aug[0:TOP, h, tile], q_aug[u][0:TOP, h, :], start=True, stop=False)
                        for qt in range(QT):
                            pe.matmul(dst[:, qt * P:(qt + 1) * P], neg[u][:, qt, tile], ident_bf[:, :], start=False, stop=False)
                        last = pe.matmul(dst, k_aug[TOP:TOP + 3, h, tile], q_aug[u][TOP:TOP + 3, h, :], start=False, stop=True)
                    last.then_inc(s_ready, 1)

            def apply(c, g, t, n, u):
                mine_dve = sum(x <= t for x in C.DVE_TILES)
                pe.wait_ge(exp_ready, n * 2 + 4)
                if t in C.DVE_TILES:
                    pe.wait_ge(gated_dve, c * N_DVE + mine_dve)
                else:
                    pe.wait_ge(gated_pool, c * N_POOL + (t + 1 - mine_dve))
                if t == 0:
                    pe.wait_ge(o_copied, c + 1)
                for j in range(HG):
                    h = HG * g + j
                    last = pe.matmul(ps_o[32 * j:32 * j + 32, :], values[u][:, t, (DH + 1) * h:(DH + 1) * h + 32],
                                     weights[(g * KT + t) % RING][:, j, :], start=(t == 0), stop=(t == KT - 1))
                last.then_inc(applied, 1)

            def job(J, name, b, u, c=None):
                k = int(name[-1]) if name[-1].isdigit() else 0
                if name in ("f0", "f5"):
                    pe.wait_ge(gate_loaded, b * 16 + 16)
                if name == "ctx0":
                    pe.wait_ge(ctx_loaded, b * 32 + 32)
                if name == "x1":
                    pe.wait_ge(x1_loaded[u], b * 8 + (16 - 8 * u))
                if name == "count":
                    pe.wait_ge(neg_made, b * (2 * QT) + 2 * QT)
                if name == "total":
                    pe.wait_ge(seen_ready, b + 1)
                if name == "row":
                    pe.wait_ge(row_ready, b + 1)
                if name == "top":
                    pe.wait_ge(top_ready, c + 1)
                if name[:3] == "den":
                    pe.wait_ge(o_copied, c + 2)
                if name == "out":
                    pe.wait_ge(o_normed, c + 1)
                pe.wait_ge(misc_read, J)
                if name[0] == "f":
                    for j in range(2 if k < 6 else 1):
                        for qt in range(QT):
                            w = P if k < 6 else REST
                            at = (QT * j + qt) * P
                            last = pe.transpose(ps_misc[0:w, at:at + P], nat[:, qt, (2 * k + j) * P:(2 * k + j) * P + w], ident[:, :])
                elif name[:3] == "ctx":
                    for j in range(4 if k < 3 else 1):
                        w = P if k < 3 else REST
                        last = pe.transpose(ps_misc[:, j * P:j * P + w], ctx_nat[0:w, 4 * k + j, :], ident[0:w, 0:w])
                elif name == "x1":
                    for qt in range(QT):
                        last = pe.transpose(ps_misc[:, qt * P:(qt + 1) * P], x1_nat[u][:, qt, :], ident[:, :])
                elif name[0] == "k":
                    n = PK // 4
                    last = pe.matmul(ps_misc[:, 0:n], w_sb[:, 1, :], ctx_T[:, n * k:n * k + n], start=True, stop=True)
                elif name == "q":
                    last = pe.matmul(ps_misc[:, 0:SQ], w_sb[:, 0, :], x1_T[:, :], start=True, stop=True)
                elif name[0] == "v":
                    for j in range(4 if k < KT // 4 else KT % 4):
                        last = pe.matmul(ps_misc[:, j * P:(j + 1) * P], ctx_T[:, (4 * k + j) * P:(4 * k + j + 1) * P], wv_sb[:, :],
                                         start=True, stop=True)
                elif name == "count":
                    for t in range(KT):
                        for qt in range(QT):
                            last = pe.matmul(ps_misc[:, t:t + 1], neg[u][:, qt, t * P:(t + 1) * P], ones_bf[:, :],
                                             start=(qt == 0), stop=(qt == QT - 1))
                elif name == "total":
                    last = pe.matmul(ps_misc[:, 0:2], ones[:, :], seen_n[:, :], start=True, stop=True)
                elif name == "row":
                    last = pe.transpose(ps_misc[0:2 * HG * KT, 0:P], row_c[:, :, :].rearrange("p h t -> p (h t)"), ident[:, :])
                elif name == "top":
                    last = pe.transpose(ps_misc[0:HG * QT, 0:P], top[:, :], ident[:, :])
                elif name[:3] == "den":
                    last = pe.matmul(ps_misc[:, 0:SQ], spread[:, :], o_sb[:, SQ:], start=True, stop=True)
                elif name == "out":
                    for qt in range(QT):
                        for g in range(G):
                            last = pe.matmul(ps_misc[:, qt * D:(qt + 1) * D], o_T[:, g, qt * P:(qt + 1) * P], wo_sb[:, g, :],
                                             start=(g == 0), stop=(g == G - 1))
                last.then_inc(misc_ready, 1)

            def prologue():
                pe.sem_inc(applied, RING)
                pe.wait_ge(made, 5)
                for J, name in enumerate(PREPARE):
                    if name == "x1":
                        pe.wait_ge(w_loaded, 16 * (7 + HG))
                        pe.wait_ge(set_dve, 6)
                        for n in range(2):
                            last = pe.matmul(ps_o[:, n:n + 1], b_perm[:, n, :], ones[0:1, 0:1], start=True, stop=True)
                        last.then_inc(b_turned, 1)
                    if name == "count":
                        pe.wait_ge(set_dve, N_SET)
                    if name == "f0":
                        pe.wait_ge(made, 8)
                    if name[0] == "f":
                        for k in range(3 * int(name[1]), 3 * int(name[1]) + 3):
                            unit(0, 0, 0, k)
                    if name == "top":
                        unit(0, 0, 0, UNITS - 1)
                    job(J, name, 0, 0, 0)

            def outline(b, u, jobs, is_first, is_last, general_way):
                for g, t, n, todo in walk(jobs, b, is_first):
                    ahead = (b, g + 1, u) if g < G - 1 else (b + 1, 0, 1 - u)
                    scores(b, g, t, n, u, general_way)
                    if not (is_last and g == G - 1):
                        for k in C.SWEEPS[t][0:1]:
                            unit(*ahead, k)
                    for J, name in todo:
                        if name in ("f5", "f6"):
                            job(J, name, b, u)
                        elif name == "top":
                            job(J, name, None, None, b * G + (g + 1))
                        elif name[:3] == "den":
                            job(J, name, None, None, b * G + (g - 1))
                        elif name == "out":
                            job(J, name, None, None, b * G - 1)
                        else:
                            job(J, name, b + 1, 1 - u)
                    if not (is_last and g == G - 1):
                        for k in C.SWEEPS[t][1:]:
                            unit(*ahead, k)
                    back = g * KT + t - LAG
                    if back >= 0:
                        apply(b * G + back // KT, back // KT, back % KT, n - LAG, u)
                    elif not is_first:
                        apply(b * G - 1, G - 1, KT + back, n - LAG, 1 - u)

            def cycle(b, u, jobs, is_first, is_last):
                pe.wait_ge(general_made, b + 1)
                pass_wait(pe, passed)
                any_mask = pe.value_load(general[u][0:1, 0:1])
                with pe.If_eq(pe.to_reg(any_mask), 0):
                    outline(b, u, jobs, is_first, is_last, False)
                with pe.Else():
                    outline(b, u, jobs, is_first, is_last, True)

            def epilogue():
                for back in range(LAG):
                    apply(B * G - 1, G - 1, KT - LAG + back, B * SLOTS - LAG + back, (B - 1) % 2)
                job(END_JOB, "den3", None, None, B * G - 1)
                job(END_JOB + 1, "out", None, None, B * G - 1)

            cycles(pe, prologue, cycle, epilogue)


def experts_pass(nc, y2_dram, router_W, router_b, sW1, sb1, sW2, sb2, eW1, eb1, eW2, eb2, out):
    E, D, H = eW1.shape
    K = 3
    chunks = y2_dram.shape[0] // CH
    JOBS = E + 1
    y2_t = y2_dram.rearrange("(c t p) d -> c p t d", t=TT, p=P)
    out_t = out.rearrange("b l d -> (b l) d").rearrange("(c t p) d -> c p t d", t=TT, p=P)

    with Scope(nc, "moe") as s:
        ident = s.sb("ident", [P, P])
        earlier = s.sb("earlier", [P, E, E])
        w1 = s.sb("w1", [P, JOBS, H])
        w2 = s.sb("w2", [P, JOBS, D])
        b1_rows = s.sb("b1_rows", [JOBS, H])
        b1 = s.sb("b1", [P, JOBS])
        b2 = s.sb("b2", [E, D])
        b2_shared = s.sb("b2_shared", [P, D])
        w_router = s.sb("w_router", [P, E])
        b_router = s.sb("b_router", [P, E])
        eps = s.sb("eps", [P, 1])
        yin = [s.sb(f"yin{u}", [P, TT, D]) for u in range(2)]
        x2 = s.sb("x2", [P, TT, D])
        acc = [s.sb(f"acc{u}", [P, TT, D]) for u in range(2)]
        x2T = [s.sb(f"x2T{u}", [P, CH]) for u in range(2)]
        cw = [s.sb(f"cw{u}", [P, TT, E]) for u in range(2)]
        cwT = [s.sb(f"cwT{u}", [E, CH]) for u in range(2)]
        hT = [s.sb(f"hT{u}", [P, CH]) for u in range(2)]
        res = [s.sb(f"res{u}", [P, TT, D]) for u in range(2)]
        stats = s.sb("stats", [P, TT, 6])
        mv = s.sb("mv", [P, TT, 2])
        std = s.sb("std", [P, TT])
        rstd = s.sb("rstd", [P, TT])
        stats2 = s.sb("stats2", [P, TT, 6])
        mv2 = s.sb("mv2", [P, TT, 2])
        std2 = s.sb("std2", [P, TT])
        rstd2 = s.sb("rstd2", [P, TT])
        logit = s.sb("logit", [P, TT, E])
        peak = s.sb("peak", [P, TT])
        shifted = s.sb("shifted", [P, TT, E])
        expd = s.sb("expd", [P, TT, E])
        total = s.sb("total", [P, TT])
        inv_total = s.sb("inv_total", [P, TT])
        prob = s.sb("prob", [P, TT, E])
        above = s.sb("above", [P, TT, E, E])
        tied = s.sb("tied", [P, TT, E, E])
        rank = s.sb("rank", [P, TT, E])
        ps_x = s.ps("ps_x", [P, CH])
        ps_r = s.ps("ps_r", [P, 512])
        ps_h = [s.ps(f"ps_h{u}", [P, CH]) for u in range(2)]
        ps_y = [s.ps(f"ps_y{u}", [P, CH]) for u in range(2)]
        ps_acc = s.ps("ps_acc", [P, CH])

        small_loaded = s.sem("small_loaded")
        w_loaded, y_loaded = s.sem("w_loaded"), [s.sem(f"y_loaded{u}") for u in range(2)]
        zeroed, ident_made, set_up = s.sem("zeroed"), s.sem("ident_made"), s.sem("set_up")
        passed = s.sem("passed")
        b1_ready, b1_copied = s.sem("b1_ready"), s.sem("b1_copied")
        yin_free = s.sem("yin_free")
        step, fin_step = s.sem("step"), s.sem("fin_step")
        var_ready, std_ready, x2_ready = s.sem("var_ready"), s.sem("std_ready"), s.sem("x2_ready")
        x2T_ready, x2T_copied = s.sem("x2T_ready"), s.sem("x2T_copied")
        router_ready, shifted_ready, exp_ready = s.sem("router_ready"), s.sem("shifted_ready"), s.sem("exp_ready")
        cw_ready, cwT_ready, cwT_copied = s.sem("cw_ready"), s.sem("cwT_ready"), s.sem("cwT_copied")
        h_ready = s.sem("h_ready")
        h_copied = s.sem("h_copied")
        o_ready = s.sem("o_ready")
        o_read = s.sem("o_read")
        var2_ready, std2_ready = s.sem("var2_ready"), s.sem("std2_ready")
        above_ready, rank_ready = s.sem("above_ready"), s.sem("rank_ready")
        res_ready, res_free = s.sem("res_ready"), s.sem("res_free")
        stored = [s.sem(f"stored{u}") for u in range(2)]
        block = s.stack.enter_context(nc.Block())
        loads = [(w1[:, 0:E, :], eW1.rearrange("e d h -> d e h")), (w1[:, E, :], sW1),
                 (w2[:, 0:E, :], eW2.rearrange("e h d -> h e d")), (w2[:, E, :], sW2),
                 (b1_rows[0:E, :], eb1), (b1_rows[E:JOBS, :], sb1.rearrange("(a h) -> a h", a=1)),
                 (b2[:, :], eb2), (b2_shared[:, :], row_bcast(sb2)), (w_router[:, :], router_W),
                 (b_router[:, :], row_bcast(router_b))]
        big, small = loads[:4], loads[4:]
        PAIRS = chunks // 2 - 1

        @block.sync
        def _(sp):
            with sp.Fori(0, chunks // 2) as i:
                for u in range(2):
                    c = i * 2 + u
                    sp.wait_ge(yin_free, c + 1)
                    sp.dma_start(yin[u][:, :, :], y2_t[bass.ds(c, 1)].rearrange("c p t d -> (c p) t d")).then_inc(y_loaded[u], 16)

        @block.gpsimd
        def _(pool):
            make_identity(pool, ident, zeroed, ident_made)
            pool.memset(eps[:, :], EPS).then_inc(set_up, 1)
            pool.memset(earlier[:, :, :], 1.0).then_inc(set_up, 1)
            pool.wait_ge(set_up, 2)
            pool.affine_select(out=earlier[:, :, :], in_=earlier[:, :, :], compare_op=ALU.is_gt, fill=0.0,
                               base=0, pattern=[[1, E], [-1, E]], channel_multiplier=0).then_inc(set_up, 1)
            pool.sem_inc(res_free, 2)
            with pool.Fori(0, chunks // 2) as i:
                for u in range(2):
                    c = i * 2 + u
                    pool.wait_ge(res_ready, c + 1)
                    pool.dma_start(out_t[bass.ds(c, 1)].rearrange("c p t d -> (c p) t d"), res[u][:, :, :]).then_inc(stored[u], 16)
                    pool.wait_ge(stored[u], i * 16 + 16)
                    pool.sem_inc(res_free, 1)

        @block.tensor
        def _(pe):
            def hidden(n, e, u):
                pe.wait_ge(h_copied, n + 1)
                pe.matmul(ps_h[e % 2][:, :], w1[:, e, :], x2T[u][:, :], start=True, stop=True).then_inc(h_ready, 1)

            def second(n, e, u):
                pe.wait_ge(h_copied, n + 3)
                pe.wait_ge(o_read, n + 1)
                dst = ps_y[e % 2] if e < E else ps_acc
                for t in range(TT):
                    tile = slice(t * P, (t + 1) * P)
                    last = pe.matmul(dst[:, tile], hT[e % 2][:, tile], w2[:, e, :], start=True, stop=e < E)
                    if e == E:
                        last = pe.matmul(dst[:, tile], cwT[u][:, tile], b2[:, :], start=False, stop=True)
                last.then_inc(o_ready, 1)

            def turn_x2(c, u):
                pe.wait_ge(x2_ready, c + 1)
                for t in range(TT):
                    last = pe.transpose(ps_x[:, t * P:(t + 1) * P], x2[:, t, :], ident[:, :])
                last.then_inc(x2T_ready, 1)

            def route(c, u):
                pe.wait_ge(x2T_copied, c + 1)
                for t in range(TT):
                    last = pe.matmul(ps_r[:, t * E:(t + 1) * E], x2T[u][:, t * P:(t + 1) * P], w_router[:, :],
                                     start=True, stop=True)
                last.then_inc(router_ready, 1)

            def turn_cw(c, u):
                pe.wait_ge(cw_ready, c + 1)
                for t in range(TT):
                    last = pe.transpose(ps_x[0:E, t * P:(t + 1) * P], cw[u][:, t, :], ident[:, :])
                last.then_inc(cwT_ready, 1)

            def chunk(c, u, prepare):
                for e in range(JOBS):
                    if e + 1 < JOBS:
                        hidden(c * JOBS + (e + 1), e + 1, u)
                    elif prepare:
                        hidden(c * JOBS + JOBS, 0, 1 - u)
                    second(c * JOBS + e, e, u)
                    if e == 3:
                        turn_cw(c, u)
                    if e == 7:
                        pe.wait_ge(cwT_copied, c + 1)
                    if prepare and e == 7:
                        turn_x2(c + 1, 1 - u)
                    if prepare and e == 8:
                        route(c + 1, 1 - u)

            pe.wait_ge(small_loaded, 16 * len(small))
            pe.wait_ge(ident_made, 1)
            pe.transpose(ps_x[:, 0:JOBS], b1_rows[:, :], ident[0:JOBS, 0:JOBS]).then_inc(b1_ready, 1)
            pe.wait_ge(b1_copied, 1)
            turn_x2(0, 0)
            route(0, 0)
            pe.wait_ge(w_loaded, 16 * len(big))
            hidden(0, 0, 0)
            chunk(0, 0, True)
            with pe.Fori(0, PAIRS) as i:
                for u in range(2):
                    chunk(i * 2 + (1 + u), 1 - u, True)
            chunk(chunks - 1, 1, False)

        @block.scalar
        def _(act):
            def relu(n, e):
                act.wait_ge(h_ready, n + 1)
                act.wait_ge(o_ready, n + 1)
                act.activation(hT[e % 2][:, :], ps_h[e % 2][:, :], ACT.Relu, bias=b1[:, e:e + 1]).then_inc(h_copied, 1)

            def root_x2(c):
                act.wait_ge(var_ready, c + 1)
                act.activation(std[:, :], mv[:, :, 1], ACT.Sqrt, bias=eps[:, :]).then_inc(std_ready, 1)

            def copy_x2T(c, u):
                act.wait_ge(x2T_ready, c + 1)
                act.activation(x2T[u][:, :], ps_x[:, :], ACT.Copy).then_inc(x2T_copied, 1)

            def exponent(c):
                act.wait_ge(shifted_ready, c + 1)
                act.activation(expd[:, :, :], shifted[:, :, :], ACT.Exp).then_inc(exp_ready, 1)

            def copy_cwT(c, u):
                act.wait_ge(cwT_ready, c + 1)
                act.activation(cwT[u][:, :], ps_x[0:E, :], ACT.Copy).then_inc(cwT_copied, 1)

            def root_sum(c):
                act.wait_ge(var2_ready, c + 1)
                act.activation(std2[:, :], mv2[:, :, 1], ACT.Sqrt, bias=eps[:, :]).then_inc(std2_ready, 1)

            def chunk(c, u, prepare, first=False):
                for e in range(JOBS):
                    relu(c * JOBS + e, e)
                    if e == 3 and not first:
                        root_sum(c - 1)
                    if prepare and e == 4:
                        root_x2(c + 1)
                    if e == 5:
                        copy_cwT(c, u)
                    if prepare and e == 8:
                        copy_x2T(c + 1, 1 - u)
                    if prepare and e == 11:
                        exponent(c + 1)

            for dst, src in small:
                act.dma_start(dst, src).then_inc(small_loaded, 16)
            for dst, src in big:
                act.dma_start(dst, src).then_inc(w_loaded, 16)
            act.sem_inc(h_copied, 2)
            act.sem_inc(o_ready, 2)
            act.wait_ge(set_up, 1)
            root_x2(0)
            act.wait_ge(b1_ready, 1)
            act.activation(b1[:, :], ps_x[:, 0:JOBS], ACT.Copy).then_inc(b1_copied, 1)
            act.wait_ge(b1_copied, 1)
            copy_x2T(0, 0)
            exponent(0)
            chunk(0, 0, True, first=True)
            with act.Fori(0, PAIRS) as i:
                for u in range(2):
                    chunk(i * 2 + (1 + u), 1 - u, True)
            chunk(chunks - 1, 1, False)
            root_sum(chunks - 1)

        @block.vector
        def _(dve):
            PREP = 11

            def over(ap, n):
                return ap.unsqueeze(2).to_broadcast([P, TT, n])

            def variance(c, u, base):
                dve.wait_ge(y_loaded[u], c * 8 + (16 - 8 * u))
                for t in range(TT):
                    last = dve.bn_stats(stats[:, t, :], yin[u][:, t, :])
                last.then_inc(step, 1)
                dve.wait_ge(step, base + 1)
                pass_wait(dve, passed)
                for t in range(TT):
                    last = dve.bn_aggr(mv[:, t, :], stats[:, t, :])
                last.then_inc(var_ready, 1)

            def normalize(c, u, base):
                dve.wait_ge(std_ready, c + 1)
                dve.reciprocal(rstd[:, :], std[:, :]).then_inc(step, 1)
                dve.wait_ge(step, base + 2)
                for t in range(TT):
                    last = dve.tensor_scalar(x2[:, t, :], yin[u][:, t, :], mv[:, t, 0:1], rstd[:, t:t + 1],
                                             ALU.subtract, ALU.mult)
                last.then_inc(x2_ready, 1)
                dve.wait_ge(x2_ready, c + 1)
                dve.tensor_tensor(acc[u][:, :, :], x2[:, :, :], b2_shared[:, :].unsqueeze(1).to_broadcast([P, TT, D]),
                                  ALU.add).then_inc(step, 1)
                dve.sem_inc(yin_free, 1)

            def shift(c, base):
                dve.wait_ge(router_ready, c + 1)
                dve.tensor_tensor(logit[:, :, :], ps_r[:, 0:TT * E].rearrange("p (t e) -> p t e", t=TT),
                                  b_router[:, :].unsqueeze(1).to_broadcast([P, TT, E]), ALU.add).then_inc(step, 1)
                dve.wait_ge(step, base + 4)
                dve.tensor_reduce(peak[:, :], logit[:, :, :], AX_X, ALU.max).then_inc(step, 1)
                dve.wait_ge(step, base + 5)
                dve.tensor_tensor(shifted[:, :, :], logit[:, :, :], over(peak[:, :], E), ALU.subtract).then_inc(shifted_ready, 1)

            def weigh(c, u, base, stage):
                other = prob[:, :, :].unsqueeze(2).to_broadcast([P, TT, E, E])
                own = prob[:, :, :].unsqueeze(3).to_broadcast([P, TT, E, E])
                if stage == 0:
                    dve.wait_ge(exp_ready, c + 1)
                    dve.tensor_reduce(total[:, :], expd[:, :, :], AX_X, ALU.add).then_inc(step, 1)
                    dve.wait_ge(step, base + 6)
                    dve.reciprocal(inv_total[:, :], total[:, :]).then_inc(step, 1)
                    dve.wait_ge(step, base + 7)
                    dve.tensor_tensor(prob[:, :, :], expd[:, :, :], over(inv_total[:, :], E), ALU.mult).then_inc(step, 1)
                if stage == 1:
                    dve.wait_ge(step, base + 8)
                    dve.tensor_tensor(tied[:, :, :, :], other, own, ALU.is_equal).then_inc(step, 1)
                if stage == 2:
                    dve.tensor_tensor(above[:, :, :, :], other, own, ALU.is_gt).then_inc(step, 1)
                if stage == 3:
                    dve.wait_ge(step, base + 9)
                    for t in range(TT):
                        last = dve.tensor_tensor(tied[:, t, :, :], tied[:, t, :, :], earlier[:, :, :], ALU.mult)
                    last.then_inc(step, 1)
                if stage == 4:
                    dve.wait_ge(step, base + 11)
                    dve.tensor_tensor(above[:, :, :, :], above[:, :, :, :], tied[:, :, :, :], ALU.add).then_inc(above_ready, 1)
                if stage == 5:
                    dve.wait_ge(above_ready, c + 1)
                    dve.tensor_reduce(rank[:, :, :], above[:, :, :, :], AX_X, ALU.add).then_inc(rank_ready, 1)
                    dve.wait_ge(rank_ready, c + 1)
                    dve.scalar_tensor_tensor(out=cw[u][:, :, :], in0=rank[:, :, :], scalar=float(K), in1=prob[:, :, :],
                                             op0=ALU.is_lt, op1=ALU.mult).then_inc(cw_ready, 1)

            def variance_sum(c, u):
                dve.wait_ge(o_read, c * JOBS + (JOBS + 2))
                for t in range(TT):
                    last = dve.bn_stats(stats2[:, t, :], acc[u][:, t, :])
                last.then_inc(fin_step, 1)
                dve.wait_ge(fin_step, c * 2 + 1)
                pass_wait(dve, passed)
                for t in range(TT):
                    last = dve.bn_aggr(mv2[:, t, :], stats2[:, t, :])
                last.then_inc(var2_ready, 1)

            def normalize_sum(c, u):
                dve.wait_ge(std2_ready, c + 1)
                dve.reciprocal(rstd2[:, :], std2[:, :]).then_inc(fin_step, 1)
                dve.wait_ge(fin_step, c * 2 + 2)
                dve.wait_ge(res_free, c + 1)
                for t in range(TT):
                    last = dve.tensor_scalar(res[u][:, t, :], acc[u][:, t, :], mv2[:, t, 0:1], rstd2[:, t:t + 1],
                                             ALU.subtract, ALU.mult)
                last.then_inc(res_ready, 1)

            def chunk(c, u, prepare, first=False):
                ahead = c * PREP + PREP
                dve.wait_ge(cw_ready, c + 1)
                for e in range(E):
                    n = c * JOBS + e
                    dve.wait_ge(o_ready, n + 3)
                    if e:
                        dve.wait_ge(o_read, n + 2)
                    for t in range(TT):
                        last = dve.scalar_tensor_tensor(out=acc[u][:, t, :], in0=ps_y[e % 2][:, t * P:(t + 1) * P],
                                                        scalar=cw[u][:, t, e:e + 1], in1=acc[u][:, t, :],
                                                        op0=ALU.mult, op1=ALU.add)
                    last.then_inc(o_read, 1)
                    if e == 0 and not first:
                        variance_sum(c - 1, 1 - u)
                    if prepare and e == 1:
                        variance(c + 1, 1 - u, ahead)
                    if e == 3 and not first:
                        normalize_sum(c - 1, 1 - u)
                    if prepare and e == 4:
                        normalize(c + 1, 1 - u, ahead)
                    if prepare and e == 8:
                        shift(c + 1, ahead)
                    if prepare and e >= 10:
                        weigh(c + 1, 1 - u, ahead, e - 10)
                n = c * JOBS + E
                dve.wait_ge(o_ready, n + 3)
                dve.wait_ge(o_read, n + 2)
                dve.tensor_tensor(acc[u][:, :, :], acc[u][:, :, :], ps_acc[:, :].rearrange("p (t d) -> p t d", t=TT),
                                  ALU.add).then_inc(o_read, 1)
                if prepare:
                    weigh(c + 1, 1 - u, ahead, 5)

            dve.sem_inc(yin_free, 2)
            dve.sem_inc(o_read, 2)
            variance(0, 0, 0)
            dve.wait_ge(small_loaded, 16 * len(small))
            dve.wait_ge(set_up, 3)
            normalize(0, 0, 0)
            shift(0, 0)
            for stage in range(6):
                weigh(0, 0, 0, stage)
            chunk(0, 0, True, first=True)
            with dve.Fori(0, PAIRS) as i:
                for u in range(2):
                    chunk(i * 2 + (1 + u), 1 - u, True)
            chunk(chunks - 1, 1, False)
            variance_sum(chunks - 1, 1)
            normalize_sum(chunks - 1, 1)


_INS = ["x", "ctx_1024", "fside_BxSxS2_0", "mask_BxSxS2_ik1"] + ["L0_attn_" + n for n in
        ("W_qkv", "b_qkv", "W_out", "b_out", "weight_q", "weight_v")] + ["L0_xattn_" + n for n in
        ("wq_k", "wq_b", "wk_k", "wk_b", "wv_k", "wv_b", "wo_k", "wo_b")] + ["L0_ffn_" + n for n in
        ("router_W", "router_b", "sW1", "sb1", "sW2", "sb2", "eW1", "eb1", "eW2", "eb2")]


def decoder_layer(nc, a, out, scratch_kind="Internal"):
    B, L, D = a["x"].shape
    x1_dram = nc.dram_tensor("x1_dram", [B * L, D], F32, kind=scratch_kind).ap()
    x2_dram = nc.dram_tensor("x2_dram", [B * L, D], F32, kind=scratch_kind).ap()
    wavelet_pass(nc, a["x"], *[a["L0_attn_" + n] for n in ("W_qkv", "b_qkv", "W_out", "b_out", "weight_q", "weight_v")], x1_dram)
    cross_pass(nc, a["ctx_1024"], a["fside_BxSxS2_0"], a["mask_BxSxS2_ik1"],
               *[a["L0_xattn_" + n] for n in ("wq_k", "wq_b", "wk_k", "wk_b", "wv_k", "wv_b", "wo_k", "wo_b")], x1_dram, x2_dram)
    experts_pass(nc, x2_dram, *[a["L0_ffn_" + n] for n in ("router_W", "router_b", "sW1", "sb1", "sW2", "sb2",
                                                           "eW1", "eb1", "eW2", "eb2")], out)


def kernel(**inputs):
    import numpy as _np
    import concourse.bacc as _bacc
    from concourse import mybir as _mybir
    from concourse.bass_utils import run_bass_kernel_spmd as _run

    nc = _bacc.Bacc("TRN2", target_bir_lowering=False, num_devices=1)
    arrays, args = {}, {}
    for name in _INS:
        a = _np.ascontiguousarray(inputs[name])
        arrays[f"in_{name}_dram"] = a
        args[name] = nc.dram_tensor(f"in_{name}_dram", a.shape, _mybir.dt.from_np(a.dtype), kind="ExternalInput").ap()
    out = nc.dram_tensor("out_0_dram", inputs["x"].shape, _mybir.dt.float32, kind="ExternalOutput").ap()
    decoder_layer(nc, args, out)
    r = _run(nc, [arrays], core_ids=[0])
    return r.results[0]["out_0_dram"]
```
